# Optimizing a Trainium2 kernel written in Bass

```python
import numpy as np
import jax
import jax.numpy as jnp

def _softmax(x, axis=-1):
    return jax.nn.softmax(x, axis=axis)

def _gelu(x):
    return jax.nn.gelu(x, approximate=True)

def _silu(x):
    return jax.nn.silu(x)

def _sigmoid(x):
    return jax.nn.sigmoid(x)

def _layernorm(x, axis=-1, eps=1e-05):
    m = jnp.mean(x, axis=axis, keepdims=True)
    v = jnp.var(x, axis=axis, keepdims=True)
    return (x - m) / jnp.sqrt(v + eps)

def _scatter_add(tgt, idx, src, axis=0):
    return tgt.at[idx].add(src)

def _segment_sum(src, seg, n):
    return jax.ops.segment_sum(src, seg, n)
kernel_name = 'mk_flamingo_gated_d2_seqx_r4_34f6e3'

def setup_inputs(seed: int=0):
    np.random.seed(seed)
    _w = jnp.asarray

    def _rec_inputs():
        import jax
        import jax.numpy as jnp
        _rk = jax.random.key(seed)
        x = -0.0003929 + 0.9999 * jax.random.normal(jax.random.fold_in(_rk, 1), (4, 512, 512), jnp.float32)
        _lenS = 512 - jax.random.randint(jax.random.fold_in(_rk, 7), (4,), 0, max(1, 512 // 4) + 1, jnp.int32)
        _lenS2 = 512 - jax.random.randint(jax.random.fold_in(_rk, 8), (4,), 0, max(1, 512 // 4) + 1, jnp.int32)
        _ctx_2048P = jax.random.normal(jax.random.fold_in(_rk, 11), (4, 16, 512), jnp.float32)
        _ctx_2048c = jax.random.dirichlet(jax.random.fold_in(_rk, 511), 0.3 * jnp.ones((16,), jnp.float32), (4, 512))
        _ctx_2048t = jnp.einsum('bsk,bkd->bsd', _ctx_2048c, _ctx_2048P)
        _ctx_2048t = _ctx_2048t * jax.lax.rsqrt(jnp.mean(jnp.square(_ctx_2048t)) + 1e-12) * 0.953939
        ctx_2048 = -0.000514642 + 1.00011 * (_ctx_2048t + 0.3 * jax.random.normal(jax.random.fold_in(_rk, 611), (4, 512, 512), jnp.float32))
        _validS = jnp.arange(512)[None, :] < _lenS[:, None]
        _validS2 = jnp.arange(512)[None, :] < _lenS2[:, None]
        _causal = jnp.tril(jnp.ones((512, 512), dtype=bool))
        mask_BxSxS2_ff0 = jnp.where(jnp.ones((4, 512, 512), dtype=bool), 0.0, -1000000000.0).astype(jnp.float32)
        _g = jax.random.normal(jax.random.fold_in(_rk, 9001), (2, 2), jnp.float32)
        _g = jnp.sign(_g) * jnp.maximum(jnp.abs(_g), 1.0) + (_g == 0) * 1.0
        g_xattn = _g[0]
        g_ffn = _g[1]
        return (x, ctx_2048, mask_BxSxS2_ff0, g_xattn, g_ffn)
    x, ctx_2048, mask_BxSxS2_ff0, g_xattn, g_ffn = _rec_inputs()

    def _L0_xattn_setup():
        import jax, jax.numpy as jnp
        import numpy as np
        NUM_HEADS = 16
        EPS = 1e-08

        def _dyn_quant(x):
            s = jnp.maximum(jnp.max(jnp.abs(x), axis=-1, keepdims=True) / 127.0, EPS)
            q = jnp.clip(jnp.round(x / s), -127.0, 127.0)
            return (q, s)

        def _quant_weight(w):
            s = jnp.maximum(jnp.max(jnp.abs(w), axis=1, keepdims=True) / 127.0, EPS)
            q = jnp.clip(jnp.round(w / s), -127.0, 127.0)
            return (q, s)

        def _w8a8_linear(x, w, b):
            qx, sx = _dyn_quant(x)
            qw, sw = _quant_weight(w)
            y = jnp.einsum('bnc,oc->bno', qx, qw) * (sx * sw[:, 0])
            return y + b
        key = jax.random.key(seed)
        ks = jax.random.split(key, 9)
        B, N, L, C = (2, 1024, 128, 512)
        sc = 0.02
        return {'x': jax.random.normal(ks[0], (B, N, C), jnp.float32), 'cond': jax.random.normal(ks[1], (B, L, C), jnp.float32), 'mask': jnp.zeros((B, N, L), jnp.float32), 'wq': jax.random.normal(ks[2], (C, C), jnp.float32) * sc, 'bq': jnp.zeros((C,), jnp.float32), 'wk': jax.random.normal(ks[3], (C, C), jnp.float32) * sc, 'bk': jnp.zeros((C,), jnp.float32), 'wv': jax.random.normal(ks[4], (C, C), jnp.float32) * sc, 'bv': jnp.zeros((C,), jnp.float32), 'wo': jax.random.normal(ks[5], (C, C), jnp.float32) * sc, 'bo': jnp.zeros((C,), jnp.float32)}
    _L0_xattn_all = _L0_xattn_setup()
    _L0_xattn_in = {k: v for k, v in _L0_xattn_all.items() if k in ('wq', 'bq', 'wk', 'bk', 'wv', 'bv', 'wo', 'bo')}
    del _L0_xattn_all

    def _L0_ffn_setup():
        import jax, jax.numpy as jnp
        import numpy as np
        _FP4_LUT = jnp.array([0.0, 0.5, 1.0, 1.5, 2.0, 3.0, 4.0, 6.0, -0.0, -0.5, -1.0, -1.5, -2.0, -3.0, -4.0, -6.0], dtype=jnp.float32)
        GROUP_SIZE = 128
        EPS = 1e-06

        def _dequant_fp4(packed_i32, scales_f16, group_size):
            out_f, in_p = packed_i32.shape
            w = packed_i32.astype(jnp.uint32)
            shifts = jnp.arange(8, dtype=jnp.uint32) * 4
            nib = w[:, :, None] >> shifts & jnp.uint32(15)
            vals = _FP4_LUT[nib.astype(jnp.int32)].reshape(out_f, in_p * 8)
            s = scales_f16.astype(jnp.float32).T
            s_full = jnp.repeat(s, group_size, axis=1)
            return vals * s_full
        key = jax.random.key(seed)
        k1, k2, k3, k4, k5 = jax.random.split(key, 5)
        B, S, H, I = (4, 512, 512, 1408)
        x = jax.random.normal(k1, (B, S, H), dtype=jnp.float32)
        gate_up_packed = jax.random.randint(k2, (2 * I, H // 8), 0, 2147483647, dtype=jnp.int32)
        gate_up_scales = jax.random.uniform(k3, (H // GROUP_SIZE, 2 * I), dtype=jnp.float32).astype(jnp.float16)
        down_packed = jax.random.randint(k4, (H, I // 8), 0, 2147483647, dtype=jnp.int32)
        down_scales = jax.random.uniform(k5, (I // GROUP_SIZE, H), dtype=jnp.float32).astype(jnp.float16)
        return {'x': x, 'gate_up_packed': gate_up_packed, 'gate_up_scales': gate_up_scales, 'down_packed': down_packed, 'down_scales': down_scales}
    _L0_ffn_all = _L0_ffn_setup()
    _L0_ffn_in = {k: v for k, v in _L0_ffn_all.items() if k in ('gate_up_packed', 'gate_up_scales', 'down_packed', 'down_scales')}
    del _L0_ffn_all

    def _L1_xattn_setup():
        import jax, jax.numpy as jnp
        import numpy as np
        HIDDEN = 512
        NUM_HEADS = 16
        NUM_KV_HEADS = 4
        HEAD_DIM = 128
        ROPE_THETA = 10000.0
        EPS = 1e-06

        def rms_norm(x, w, eps=EPS):
            var = jnp.mean(jnp.square(x), axis=-1, keepdims=True)
            return x * jax.lax.rsqrt(var + eps) * w

        def rope_cache(L, head_dim, theta, dtype):
            inv_freq = 1.0 / theta ** (jnp.arange(0, head_dim, 2, dtype=jnp.float32) / head_dim)
            t = jnp.arange(L, dtype=jnp.float32)
            freqs = jnp.outer(t, inv_freq)
            emb = jnp.concatenate([freqs, freqs], -1)
            cos = jnp.cos(emb).astype(dtype)[None, :, None, :]
            sin = jnp.sin(emb).astype(dtype)[None, :, None, :]
            return (cos, sin)

        def rotate_half(x):
            x1, x2 = jnp.split(x, 2, axis=-1)
            return jnp.concatenate([-x2, x1], axis=-1)
        key = jax.random.key(seed)
        ks = jax.random.split(key, 10)
        B, L, T = (2, 512, 128)
        q_out = NUM_HEADS * HEAD_DIM
        kv_out = NUM_KV_HEADS * HEAD_DIM
        s = lambda fan_in: 1.0 / np.sqrt(fan_in)
        return {'x': jax.random.normal(ks[0], (B, L, HIDDEN), jnp.float32), 'h_ctx_kv': jax.random.normal(ks[1], (B, T, HIDDEN), jnp.float32), 'wq': jax.random.normal(ks[2], (HIDDEN, q_out), jnp.float32) * s(HIDDEN), 'wk': jax.random.normal(ks[3], (HIDDEN, kv_out), jnp.float32) * s(HIDDEN), 'wv': jax.random.normal(ks[4], (HIDDEN, kv_out), jnp.float32) * s(HIDDEN), 'wo': jax.random.normal(ks[5], (q_out, HIDDEN), jnp.float32) * s(q_out), 'wk_ctx': jax.random.normal(ks[6], (HIDDEN, kv_out), jnp.float32) * s(HIDDEN), 'wv_ctx': jax.random.normal(ks[7], (HIDDEN, kv_out), jnp.float32) * s(HIDDEN), 'q_norm_w': jnp.ones((HEAD_DIM,), jnp.float32), 'k_norm_w': jnp.ones((HEAD_DIM,), jnp.float32)}
    _L1_xattn_all = _L1_xattn_setup()
    _L1_xattn_in = {k: v for k, v in _L1_xattn_all.items() if k in ('wq', 'wk', 'wv', 'wo', 'wk_ctx', 'wv_ctx', 'q_norm_w', 'k_norm_w')}
    del _L1_xattn_all

    def _L1_ffn_setup():
        import jax, jax.numpy as jnp
        import numpy as np
        B, S, H = (2, 256, 512)
        E, K, F = (64, 8, 192)
        CAP = 128
        key = jax.random.key(seed)
        k1, k2, k3, k4, k5 = jax.random.split(key, 5)
        scale_h = 1.0 / np.sqrt(H)
        scale_f = 1.0 / np.sqrt(F)
        return {'hidden_states': jax.random.normal(k1, (B, S, H), jnp.float32), 'router_w': jax.random.normal(k2, (E, H), jnp.float32) * scale_h, 'w_gate': jax.random.normal(k3, (E, H, F), jnp.float32) * scale_h, 'w_up': jax.random.normal(k4, (E, H, F), jnp.float32) * scale_h, 'w_down': jax.random.normal(k5, (E, F, H), jnp.float32) * scale_f}
    _L1_ffn_all = _L1_ffn_setup()
    _L1_ffn_in = {k: v for k, v in _L1_ffn_all.items() if k in ('router_w', 'w_gate', 'w_up', 'w_down')}
    del _L1_ffn_all
    return {'x': x, 'ctx_2048': ctx_2048, 'mask_BxSxS2_ff0': mask_BxSxS2_ff0, 'g_xattn': g_xattn, 'g_ffn': g_ffn, 'L0_xattn_wq': _L0_xattn_in['wq'], 'L0_xattn_bq': _L0_xattn_in['bq'], 'L0_xattn_wk': _L0_xattn_in['wk'], 'L0_xattn_bk': _L0_xattn_in['bk'], 'L0_xattn_wv': _L0_xattn_in['wv'], 'L0_xattn_bv': _L0_xattn_in['bv'], 'L0_xattn_wo': _L0_xattn_in['wo'], 'L0_xattn_bo': _L0_xattn_in['bo'], 'L0_ffn_gate_up_packed': _L0_ffn_in['gate_up_packed'], 'L0_ffn_gate_up_scales': _L0_ffn_in['gate_up_scales'], 'L0_ffn_down_packed': _L0_ffn_in['down_packed'], 'L0_ffn_down_scales': _L0_ffn_in['down_scales'], 'L1_xattn_wq': _L1_xattn_in['wq'], 'L1_xattn_wk': _L1_xattn_in['wk'], 'L1_xattn_wv': _L1_xattn_in['wv'], 'L1_xattn_wo': _L1_xattn_in['wo'], 'L1_xattn_wk_ctx': _L1_xattn_in['wk_ctx'], 'L1_xattn_wv_ctx': _L1_xattn_in['wv_ctx'], 'L1_xattn_q_norm_w': _L1_xattn_in['q_norm_w'], 'L1_xattn_k_norm_w': _L1_xattn_in['k_norm_w'], 'L1_ffn_router_w': _L1_ffn_in['router_w'], 'L1_ffn_w_gate': _L1_ffn_in['w_gate'], 'L1_ffn_w_up': _L1_ffn_in['w_up'], 'L1_ffn_w_down': _L1_ffn_in['w_down']}

def reference(x, ctx_2048, mask_BxSxS2_ff0, g_xattn, g_ffn, L0_xattn_wq, L0_xattn_bq, L0_xattn_wk, L0_xattn_bk, L0_xattn_wv, L0_xattn_bv, L0_xattn_wo, L0_xattn_bo, L0_ffn_gate_up_packed, L0_ffn_gate_up_scales, L0_ffn_down_packed, L0_ffn_down_scales, L1_xattn_wq, L1_xattn_wk, L1_xattn_wv, L1_xattn_wo, L1_xattn_wk_ctx, L1_xattn_wv_ctx, L1_xattn_q_norm_w, L1_xattn_k_norm_w, L1_ffn_router_w, L1_ffn_w_gate, L1_ffn_w_up, L1_ffn_w_down):
    import jax
    import jax.numpy as jnp

    def _L0_xattn_ref(x, cond, mask, wq, bq, wk, bk, wv, bv, wo, bo):
        import jax, jax.numpy as jnp
        import numpy as np
        NUM_HEADS = 16
        EPS = 1e-08

        def _dyn_quant(x):
            s = jnp.maximum(jnp.max(jnp.abs(x), axis=-1, keepdims=True) / 127.0, EPS)
            q = jnp.clip(jnp.round(x / s), -127.0, 127.0)
            return (q, s)

        def _quant_weight(w):
            s = jnp.maximum(jnp.max(jnp.abs(w), axis=1, keepdims=True) / 127.0, EPS)
            q = jnp.clip(jnp.round(w / s), -127.0, 127.0)
            return (q, s)

        def _w8a8_linear(x, w, b):
            qx, sx = _dyn_quant(x)
            qw, sw = _quant_weight(w)
            y = jnp.einsum('bnc,oc->bno', qx, qw) * (sx * sw[:, 0])
            return y + b
        B, N, C = x.shape
        L = cond.shape[1]
        H = NUM_HEADS
        D = C // H
        inv_sqrt_d = np.float32(1.0 / np.sqrt(D))
        q = _w8a8_linear(x, wq, bq).reshape(B, N, H, D).transpose(0, 2, 1, 3)
        k = (cond @ wk.T + bk).reshape(B, L, H, D).transpose(0, 2, 1, 3)
        v = (cond @ wv.T + bv).reshape(B, L, H, D).transpose(0, 2, 1, 3)
        scores = jnp.einsum('bhnd,bhld->bhnl', q, k) * inv_sqrt_d + mask[:, None]
        attn = jax.nn.softmax(scores, axis=-1)
        o = jnp.einsum('bhnl,bhld->bhnd', attn, v)
        o = o.transpose(0, 2, 1, 3).reshape(B, N, C)
        return _w8a8_linear(o, wo, bo)

    def _L0_ffn_ref(x, gate_up_packed, gate_up_scales, down_packed, down_scales):
        import jax, jax.numpy as jnp
        import numpy as np
        _FP4_LUT = jnp.array([0.0, 0.5, 1.0, 1.5, 2.0, 3.0, 4.0, 6.0, -0.0, -0.5, -1.0, -1.5, -2.0, -3.0, -4.0, -6.0], dtype=jnp.float32)
        GROUP_SIZE = 128
        EPS = 1e-06

        def _dequant_fp4(packed_i32, scales_f16, group_size):
            out_f, in_p = packed_i32.shape
            w = packed_i32.astype(jnp.uint32)
            shifts = jnp.arange(8, dtype=jnp.uint32) * 4
            nib = w[:, :, None] >> shifts & jnp.uint32(15)
            vals = _FP4_LUT[nib.astype(jnp.int32)].reshape(out_f, in_p * 8)
            s = scales_f16.astype(jnp.float32).T
            s_full = jnp.repeat(s, group_size, axis=1)
            return vals * s_full
        I = gate_up_packed.shape[0] // 2
        w_gu = _dequant_fp4(gate_up_packed, gate_up_scales, GROUP_SIZE)
        w_down = _dequant_fp4(down_packed, down_scales, GROUP_SIZE)
        gate_up = jnp.einsum('bsh,oh->bso', x, w_gu)
        gate, up = (gate_up[..., :I], gate_up[..., I:])
        h = jax.nn.silu(gate) * up
        y = jnp.einsum('bsi,hi->bsh', h, w_down)
        rms = jnp.sqrt(jnp.mean(y * y, axis=-1, keepdims=True) + EPS)
        return y / rms

    def _L1_xattn_ref(x, h_ctx_kv, wq, wk, wv, wo, wk_ctx, wv_ctx, q_norm_w, k_norm_w):
        import jax, jax.numpy as jnp
        import numpy as np
        HIDDEN = 512
        NUM_HEADS = 16
        NUM_KV_HEADS = 4
        HEAD_DIM = 128
        ROPE_THETA = 10000.0
        EPS = 1e-06

        def rms_norm(x, w, eps=EPS):
            var = jnp.mean(jnp.square(x), axis=-1, keepdims=True)
            return x * jax.lax.rsqrt(var + eps) * w

        def rope_cache(L, head_dim, theta, dtype):
            inv_freq = 1.0 / theta ** (jnp.arange(0, head_dim, 2, dtype=jnp.float32) / head_dim)
            t = jnp.arange(L, dtype=jnp.float32)
            freqs = jnp.outer(t, inv_freq)
            emb = jnp.concatenate([freqs, freqs], -1)
            cos = jnp.cos(emb).astype(dtype)[None, :, None, :]
            sin = jnp.sin(emb).astype(dtype)[None, :, None, :]
            return (cos, sin)

        def rotate_half(x):
            x1, x2 = jnp.split(x, 2, axis=-1)
            return jnp.concatenate([-x2, x1], axis=-1)
        B, L, _ = x.shape
        T = h_ctx_kv.shape[1]
        rep = NUM_HEADS // NUM_KV_HEADS
        q = (x @ wq).reshape(B, L, NUM_HEADS, HEAD_DIM)
        k = (x @ wk).reshape(B, L, NUM_KV_HEADS, HEAD_DIM)
        v = (x @ wv).reshape(B, L, NUM_KV_HEADS, HEAD_DIM)
        q = rms_norm(q, q_norm_w)
        k = rms_norm(k, k_norm_w)
        k_ctx = (h_ctx_kv @ wk_ctx).reshape(B, T, NUM_KV_HEADS, HEAD_DIM)
        v_ctx = (h_ctx_kv @ wv_ctx).reshape(B, T, NUM_KV_HEADS, HEAD_DIM)
        k_ctx = rms_norm(k_ctx, k_norm_w)
        cos, sin = rope_cache(L, HEAD_DIM, ROPE_THETA, x.dtype)
        q = q * cos + rotate_half(q) * sin
        k = k * cos + rotate_half(k) * sin
        k_full = jnp.concatenate([k_ctx, k], axis=1)
        v_full = jnp.concatenate([v_ctx, v], axis=1)
        k_full = jnp.repeat(k_full, rep, axis=2)
        v_full = jnpp_repeat = jnp.repeat(v_full, rep, axis=2)
        i = jnp.arange(L)[:, None]
        j = jnp.arange(L)[None, :]
        causal = jnp.where(j > i, -jnp.inf, 0.0).astype(x.dtype)
        mask = jnp.concatenate([jnp.zeros((L, T), x.dtype), causal], axis=1)
        scale = 1.0 / np.sqrt(HEAD_DIM)
        scores = jnp.einsum('blhd,bmhd->bhlm', q, k_full) * scale + mask
        probs = jax.nn.softmax(scores, axis=-1)
        out = jnp.einsum('bhlm,bmhd->blhd', probs, v_full)
        out = out.reshape(B, L, NUM_HEADS * HEAD_DIM)
        return out @ wo

    def _L1_ffn_ref(hidden_states, router_w, w_gate, w_up, w_down):
        import jax, jax.numpy as jnp
        import numpy as np
        B, S, H = (2, 256, 512)
        E, K, F = (64, 8, 192)
        CAP = 128
        b, s, h = hidden_states.shape
        T = b * s
        xf = hidden_states.reshape(T, h)
        logits = xf @ router_w.T
        scores = jax.nn.softmax(logits.astype(jnp.float32), axis=-1)
        topk_w, topk_idx = jax.lax.top_k(scores, K)
        topk_w = topk_w / (topk_w.sum(axis=-1, keepdims=True) + 1e-20)
        slot_expert = topk_idx.reshape(-1)
        slot_token = jnp.repeat(jnp.arange(T), K)
        onehot = jax.nn.one_hot(slot_expert, E, dtype=jnp.int32)
        pos = (jnp.cumsum(onehot, axis=0) * onehot).sum(-1) - 1
        valid = pos < CAP
        dest = jnp.where(valid, slot_expert * CAP + pos, E * CAP)
        buf = jnp.zeros((E * CAP + 1, h), xf.dtype).at[dest].set(xf[slot_token])
        xb = buf[:E * CAP].reshape(E, CAP, h)
        gate = jnp.einsum('ech,ehf->ecf', xb, w_gate)
        up = jnp.einsum('ech,ehf->ecf', xb, w_up)
        hmid = jax.nn.silu(gate) * up
        yb = jnp.einsum('ecf,efh->ech', hmid, w_down).reshape(E * CAP, h)
        yb = jnp.concatenate([yb, jnp.zeros((1, h), yb.dtype)], axis=0)
        slot_out = yb[dest] * topk_w.reshape(-1)[:, None].astype(yb.dtype)
        out = jnp.zeros((T, h), yb.dtype).at[slot_token].add(slot_out)
        return out.reshape(b, s, h)
    x = x + jnp.tanh(g_xattn[0]) * _L0_xattn_ref(_layernorm(x, axis=-1), ctx_2048, mask_BxSxS2_ff0, L0_xattn_wq, L0_xattn_bq, L0_xattn_wk, L0_xattn_bk, L0_xattn_wv, L0_xattn_bv, L0_xattn_wo, L0_xattn_bo)
    x = x + jnp.tanh(g_ffn[0]) * _L0_ffn_ref(_layernorm(x, axis=-1), L0_ffn_gate_up_packed, L0_ffn_gate_up_scales, L0_ffn_down_packed, L0_ffn_down_scales)
    x = x + jnp.tanh(g_xattn[1]) * _L1_xattn_ref(_layernorm(x, axis=-1), ctx_2048, L1_xattn_wq, L1_xattn_wk, L1_xattn_wv, L1_xattn_wo, L1_xattn_wk_ctx, L1_xattn_wv_ctx, L1_xattn_q_norm_w, L1_xattn_k_norm_w)
    x = x + jnp.tanh(g_ffn[1]) * _L1_ffn_ref(_layernorm(x, axis=-1), L1_ffn_router_w, L1_ffn_w_gate, L1_ffn_w_up, L1_ffn_w_down)
    return x

_drawn_inputs = setup_inputs


def setup_inputs(seed=0):
    import zlib

    import numpy as np

    out = dict(_drawn_inputs(seed))
    spreads = {'g_ffn': (-1.0, 0.6),
     'L0_xattn_bq': (0.0, 0.8),
     'L0_xattn_bk': (0.0, 0.8),
     'L0_xattn_bv': (0.0, 0.1),
     'L0_xattn_bo': (0.0, 0.1),
     'L1_xattn_q_norm_w': (1.0, 0.538),
     'L1_xattn_k_norm_w': (1.0, 0.568)}
    factors = {'L0_xattn_wq': 4.975, 'L0_xattn_wk': 5.114}
    for name, (base, spread) in spreads.items():
        noise = np.random.default_rng([zlib.crc32(name.encode()), seed]).standard_normal(out[name].shape)
        drawn = base * np.exp(spread * noise) if base else spread * noise
        out[name] = jnp.asarray(drawn.astype(out[name].dtype))
    for name, factor in factors.items():
        out[name] = (out[name] * factor).astype(out[name].dtype)
    return out
```

```python
from contextlib import ExitStack

import numpy as np

import concourse.bass as bass
from concourse import mybir

ALU = mybir.AluOpType
ACT = mybir.ActivationFunctionType
AX = mybir.AxisListType
F32 = mybir.dt.float32
F32R = mybir.dt.float32r
BF16 = mybir.dt.bfloat16
F16 = mybir.dt.float16
I32 = mybir.dt.int32
U32 = mybir.dt.uint32

P = 128
B = 4
S = 512
D = 512
KC = D // P
NT = S // P
T = B * S
TILES = T // P
LN_EPS = 1e-5
ROUND = 1.5 * 2.0 ** 23


class Chain:

    def __init__(self, eng, sem):
        self.eng, self.sem, self.n = eng, sem, 0

    def restart(self):
        self.eng.sem_clear(self.sem)
        self.n = 0

    def __call__(self, instruction):
        self.n += 1
        instruction.then_inc(self.sem, 1)
        self.eng.wait_ge(self.sem, self.n)


def wait_apart(eng, begun, sem, value):
    eng.wait_ge(begun, 1)
    eng.wait_ge(sem, value)


def pass_wait(eng, passed, sem, value):
    eng.wait_ge(sem, value)
    eng.sem_inc(passed, 1)


def clear_all(eng, sems):
    numbers = sorted(sem.num for sem in sems)
    while numbers:
        first = numbers[0]
        run = [n for i, n in enumerate(numbers) if n == first + i]
        eng.sem_clear(range(first, first + len(run)))
        numbers = numbers[len(run):]


class Stage:
    OF_DMAS = ("loaded", "stored", "stacked", "gathered", "scattered")
    kept = []

    def __init__(self, nc, ctx, name):
        self.nc, self.ctx, self.name, self.sems = nc, ctx, name, []

    def sb(self, name, shape, dt):
        return self.ctx.enter_context(self.nc.sbuf_tensor(f"{self.name}_{name}", shape, dt))

    def ps(self, name, shape, dt):
        return self.ctx.enter_context(self.nc.psum_tensor(f"{self.name}_{name}", shape, dt))

    def sem(self, name):
        made = self.nc.semaphore(f"{self.name}_{name}")
        if any(word in name for word in self.OF_DMAS):
            self.kept.append(made)
            return made.__enter__()
        self.sems.append(self.ctx.enter_context(made))
        return self.sems[-1]

    def clear(self):
        def share(eng, k):
            quarter = -(-len(self.sems) // 4)
            clear_all(eng, self.sems[k * quarter:(k + 1) * quarter])
        with self.nc.Block() as block:

            @block.sync
            def _(sp):
                share(sp, 0)

            @block.scalar
            def _(act):
                share(act, 1)

            @block.vector
            def _(dve):
                share(dve, 2)

            @block.gpsimd
            def _(pool):
                share(pool, 3)


def rows(ap):
    return ap.rearrange("(t p) n -> p t n", p=P)


def row_of(ap, n, width):
    return bass.AP(tensor=ap.tensor, offset=ap.offset + n, ap=[[0, P], [1, width]])


def mm3(pe, out, lhsT, rhs, first, last, **kw):
    (lh, ll), (rh, rl) = lhsT, rhs
    pe.matmul(out, ll, rh, start=first, stop=False, **kw)
    pe.matmul(out, lh, rl, start=False, stop=False, **kw)
    return pe.matmul(out, lh, rh, start=False, stop=last, **kw)


H0 = 16
D0 = D // H0
SCALE0 = float(np.float32(1.0 / np.sqrt(D0)))


def layer_norm(dve, step, var_ready, rstd_ready, turn, x, m, xn):
    step(dve.bn_stats(m["stats"][:], x))
    step(dve.bn_aggr(m["mv"][:], m["stats"][:]))
    dve.tensor_scalar(m["ve"][:], m["mv"][:, 1:2], LN_EPS, None, ALU.add).then_inc(var_ready, 1)
    dve.wait_ge(rstd_ready, turn + 1)
    step(dve.tensor_scalar(xn, x, m["mv"][:, 0:1], m["rstd"][:], ALU.subtract, ALU.mult))


def norm_buffers(st):
    return {"stats": st.sb("stats", [P, 6], F32), "mv": st.sb("mv", [P, 2], F32),
            "ve": st.sb("ve", [P, 1], F32), "rstd": st.sb("rstd", [P, 1], F32)}


def quantise(dve, step, x, m, out):
    step(dve.tensor_reduce(m["amax"][:], x, AX.X, ALU.max, apply_absolute_value=True))
    step(dve.tensor_scalar(m["s"][:], m["amax"][:], float(np.float32(1 / 127)), 1e-8, ALU.mult, ALU.max))
    step(dve.reciprocal(m["sinv"][:], m["s"][:]))
    step(dve.tensor_scalar(m["scaled"][:], x, m["sinv"][:], 127.0, ALU.mult, ALU.min))
    step(dve.tensor_scalar(m["scaled"][:], m["scaled"][:], -127.0, ROUND, ALU.max, ALU.add))
    return dve.tensor_scalar(out, m["scaled"][:], ROUND, None, ALU.subtract)


def constants(st, nc):
    c = {"ident": st.sb("ident", [P, P], F32), "identb": st.sb("identb", [P, P], BF16),
         "ones": st.sb("ones", [P, P], F32), "mhalf": st.sb("mhalf", [P, 1], F32)}
    return c


def make_constants(pool, c, made):
    pool.memset(c["ident"][:], 0.0).then_inc(made, 1)
    pool.memset(c["ones"][:], 1.0).then_inc(made, 1)
    pool.memset(c["mhalf"][:], -0.5).then_inc(made, 1)
    pool.wait_ge(made, 3)
    pool.affine_select(out=c["ident"][:], in_=c["ident"][:], compare_op=ALU.not_equal, fill=1.0, base=0,
                       pattern=[[-1, P]], channel_multiplier=1).then_inc(made, 1)
    pool.wait_ge(made, 4)
    pool.tensor_copy(c["identb"][:], c["ident"][:]).then_inc(made, 1)


CONSTS = 5


def layer0_attention(nc, d, x_out):
    with ExitStack() as ctx:
        st = Stage(nc, ctx, "a0")
        sb, ps, sem = st.sb, st.ps, st.sem
        c = constants(st, nc)
        gate = sb("gate", [P, 1], F32)
        wqT = sb("wqT", [P, KC, D], BF16)
        woT = sb("woT", [P, KC, D], BF16)
        swq = sb("swq", [P, KC], F32)
        bqs = sb("bqs", [P, KC], F32)
        bk = sb("bk", [P, KC], F32)
        swo_row = sb("swo_row", [P, D], F32)
        bv_row = sb("bv_row", [P, D], F32)
        bo_row = sb("bo_row", [P, D], F32)
        wk = [sb(f"wk{i}", [P, KC, D], F32R) for i in range(2)]
        wv = [sb(f"wv{i}", [P, KC, D], F32R) for i in range(2)]
        bank = [ps(f"bank{i}", [P, 512], F32) for i in range(8)]
        misc = bank[7]
        miscb = misc[:, :].bitcast(BF16)
        prepare_layer0_weights(nc, d, c, gate, wqT, woT, swq, bqs, bk, swo_row, bv_row, bo_row, wk, wv, bank)

        x4 = sb("x4", [P, NT, D], F32)
        ctx_f = sb("ctx_f", [P, KC, S], F32)
        ctx_s = [sb(f"ctx_s{i}", [P, KC, S], F32R) for i in range(2)]
        mask_t = [sb(f"mask_t{i}", [P, S], F32) for i in range(2)]
        m = norm_buffers(st)
        for n in ("amax", "s", "sinv"):
            m[n] = sb(n, [P, 1], F32)
        m["scaled"] = sb("scaled", [P, D], F32)
        xn = sb("xn", [P, D], F32)
        qx = sb("qx", [P, D], BF16)
        diag = sb("diag", [P, P], F32)
        qxT = sb("qxT", [P, KC, S], BF16)
        sx_row = sb("sx_row", [P, S], F32)
        q_f = sb("q_f", [P, KC, S], F32)
        q_s = ctx_s
        k_s = [sb(f"k_s{i}", [P, KC, S], F32R) for i in range(2)]
        k_st = sb("k_st", [P, H0, S], F32R)
        q_st = [sb(f"q_st{i}", [P, H0, P], F32R) for i in range(2)]
        v = sb("v", [P, NT, D], F32)
        prob = sb("prob", [P, 4, S], F32)
        probT = sb("probT", [P, 2, 4 * P], F32)
        nmax = sb("nmax", [P, 4], F32)
        rsum = sb("rsum", [P, H0], F32)
        rinv = sb("rinv", [P, H0], F32)
        o = sb("o", [P, D], F32)
        qo = sb("qo", [P, D], BF16)
        oT = sb("oT", [P, KC, P], BF16)
        score, probT_ps, o_ps = bank[0:4], bank[4:6], bank[6]

        (consts_made, x_loaded, ctx_loaded, mask_loaded, var_ready, rstd_ready, x_quant, x_turned, x_copied,
         ctx_hi, ctx_lo, k_done, k_hi, k_lo, v_done, v_copied, q_done, q_fp, q_hi, q_lo, k_stacked, q_stacked,
         scored, shifted, expd, turned, copied_dve, copied_act, summed, o_quant, o_turned, o_copied, projected,
         tile_done, stored, step_dve) = (sem(n) for n in (
             "consts_made x_loaded ctx_loaded mask_loaded var_ready rstd_ready x_quant x_turned x_copied "
             "ctx_hi ctx_lo k_done k_hi k_lo v_done v_copied q_done q_fp q_hi q_lo k_stacked q_stacked "
             "scored shifted expd turned copied_dve copied_act summed o_quant o_turned o_copied projected "
             "tile_done stored step_dve").split())
        batch_stored, begun = sem("batch_stored"), sem("begun")
        q_stacked = (q_stacked, sem("q_stacked_odd"))
        mask_loaded = (mask_loaded, sem("mask_loaded_odd"))
        x_src = d["x"].rearrange("b (t p) n -> b p t n", p=P)
        mask_src = d["mask"].rearrange("b (t p) n -> (b t) p n", p=P)
        ctxT_src = d["ctxT"].rearrange("b (k p) s -> b p k s", p=P)
        x_dst = x_out.rearrange("(g p) n -> g p n", p=P)

        with nc.Block() as block:

            @block.sync
            def _(sp):
                with sp.Fori(0, B) as b:
                    wait_apart(sp, begun, batch_stored, b + 1)
                    sp.dma_start(ctx_f[:], ctxT_src[b]).then_inc(ctx_loaded, 16)
                    sp.dma_start(x4[:], x_src[b]).then_inc(x_loaded, 16)
                    wait_apart(sp, begun, k_hi, b * KC + KC)
                    wait_apart(sp, begun, k_lo, b * KC + KC)
                    for i in range(4):
                        for r in range(4):
                            sp.dma_start(
                                k_st[32 * r:32 * r + 32].bitcast(F32).rearrange("p (j i) s -> p i j s", i=4)[:, i],
                                k_s[r % 2][32 * i:32 * i + 32].bitcast(F32)).then_inc(k_stacked, 16)
                    wait_apart(sp, begun, q_hi, b + 1)
                    wait_apart(sp, begun, q_lo, b + 1)
                    with sp.Fori(0, NT // 2) as tp:
                        for u in range(2):
                            wait_apart(sp, begun, tile_done, b * NT + tp * 2 + (u + 1))
                            for i in range(4):
                                for r in range(4):
                                    sp.dma_start(
                                        q_st[u][32 * r:32 * r + 32].bitcast(F32).rearrange("p (j i) s -> p i j s", i=4)[:, i],
                                        q_s[r // 2][32 * i:32 * i + 32, :, bass.ds(tp * (2 * P) + u * P, P)].bitcast(F32)
                                    ).then_inc(q_stacked[u], 16)
                            sp.dma_start(mask_t[u][:], mask_src[b * NT + tp * 2 + u]).then_inc(mask_loaded[u], 16)

            @block.gpsimd
            def _(pool):
                pool.sem_inc(begun, 1)
                pool.sem_inc(batch_stored, 1)
                with pool.Fori(0, B) as b:
                    with pool.Fori(0, NT) as t:
                        pool.wait_ge(var_ready, b * NT + t + 1)
                        pool.tensor_tensor(m["rstd"][:], m["ve"][:], c["mhalf"][:], ALU.pow).then_inc(rstd_ready, 1)
                    with pool.Fori(0, NT) as t:
                        pool.wait_ge(tile_done, b * NT + t + 3)
                        pool.dma_start(x_dst[b * NT + t], x4[:, bass.ds(t, 1)]).then_inc(stored, 16)
                    pool.wait_ge(stored, b * (16 * NT) + 16 * NT)
                    pool.sem_inc(batch_stored, 1)

            @block.scalar
            def _(act):
                with act.Fori(0, B) as b:
                    act.wait_ge(ctx_loaded, b * 16 + 16)
                    act.activation(ctx_s[0][:], ctx_f[:], ACT.Copy).then_inc(ctx_hi, 1)
                    for j in range(KC):
                        act.wait_ge(k_done, b * KC + (j + 1))
                        act.activation(k_s[0][:, j], bank[j][:], ACT.Identity,
                                       bias=bk[:, j:j + 1]).then_inc(k_hi, 1)
                    act.wait_ge(q_fp, b + 1)
                    act.activation(q_s[0][:], q_f[:], ACT.Copy).then_inc(q_hi, 1)
                    with act.Fori(0, NT) as t:
                        for h in range(H0 + 2):
                            if h < H0:
                                act.wait_ge(shifted, h + 1)
                                act.activation(prob[:, h % 4], prob[:, h % 4], ACT.Exp,
                                               bias=nmax[:, h % 4:h % 4 + 1], scale=-1.0,
                                               accum_out=rsum[:, h:h + 1]).then_inc(expd, 1)
                            k = h - 2
                            if k >= 0 and k % 2 == 1:
                                act.wait_ge(turned, k + 1)
                                if k >= 2:
                                    act.wait_ge(summed, k - 1)
                                act.activation(probT[:, 1], probT_ps[1][:], ACT.Copy).then_inc(copied_act, 1)
                        act.wait_ge(o_quant, b * NT + t + 1)

            @block.tensor
            def _(pe):
                with pe.Fori(0, B) as b:
                    wait_apart(pe, begun, ctx_hi, b + 1)
                    wait_apart(pe, begun, ctx_lo, b + 1)
                    for j in range(KC):
                        for k in range(KC):
                            mm = mm3(pe, bank[j][:], [w[:, k, j * P:j * P + P] for w in wk],
                                     [x[:, k] for x in ctx_s], k == 0, k == KC - 1)
                        mm.then_inc(k_done, 1)
                    for l in range(NT):
                        if l >= 2:
                            wait_apart(pe, begun, v_copied, b * NT + (l - 1))
                        for k in range(KC):
                            mm = mm3(pe, bank[4 + l % 2][:], [x[:, k, l * P:l * P + P] for x in ctx_s],
                                     [w[:, k] for w in wv], k == 0, k == KC - 1)
                        mm.then_inc(v_done, 1)
                    for t in range(NT):
                        wait_apart(pe, begun, x_quant, b * NT + (t + 1))
                        if t:
                            wait_apart(pe, begun, x_copied, b * NT + t)
                        pe.matmul(o_ps[:, 0:P], c["ones"][:], diag[:], start=True, stop=True)
                        for k in range(KC):
                            mm = pe.transpose(miscb[:, k * P:k * P + P], qx[:, k * P:k * P + P], c["identb"][:])
                        mm.then_inc(x_turned, 1)
                    wait_apart(pe, begun, x_copied, b * NT + NT)
                    for j in range(KC):
                        wait_apart(pe, begun, k_lo, b * KC + (j + 1))
                        for k in range(KC):
                            mm = pe.matmul(bank[j][:], wqT[:, k, j * P:j * P + P], qxT[:, k],
                                           start=(k == 0), stop=(k == KC - 1))
                        mm.then_inc(q_done, 1)
                    wait_apart(pe, begun, q_fp, b + 1)
                    with pe.Fori(0, NT // 2) as tp:
                        for u in range(2):
                            g = b * NT + tp * 2 + u
                            wait_apart(pe, begun, k_stacked, b * 256 + 256)
                            wait_apart(pe, begun, q_stacked[u], (b * 2 + tp) * 256 + 256)
                            wait_apart(pe, begun, mask_loaded[u], (b * 2 + tp) * 16 + 16)

                            def scores(pair):
                                for h in (2 * pair, 2 * pair + 1):
                                    if h >= 4:
                                        pe.wait_ge(shifted, h - 3)
                                    pe.matmul(score[h % 4][:], q_st[u][:, h], k_st[:, h],
                                              start=True, stop=True).then_inc(scored, 1)

                            def turn(h):
                                pe.wait_ge(expd, h + 1)
                                if h >= 2:
                                    pe.wait_ge((copied_dve, copied_act)[h % 2], h // 2)
                                for l in range(NT):
                                    mm = pe.transpose(probT_ps[h % 2][:, l * P:l * P + P],
                                                      prob[:, h % 4, l * P:l * P + P], c["ident"][:])
                                mm.then_inc(turned, 1)

                            def weigh(h):
                                pe.wait_ge((copied_dve, copied_act)[h % 2], h // 2 + 1)
                                for l in range(NT):
                                    mm = pe.matmul(o_ps[:, h * D0:h * D0 + D0], probT[:, h % 2, l * P:l * P + P],
                                                   v[:, l, h * D0:h * D0 + D0], start=(l == 0), stop=(l == NT - 1))
                                mm.then_inc(summed, 1)

                            scores(0)
                            for pair in range(H0 // 2):
                                if pair + 1 < H0 // 2:
                                    scores(pair + 1)
                                turn(2 * pair)
                                if pair:
                                    weigh(2 * pair - 1)
                                turn(2 * pair + 1)
                                weigh(2 * pair)
                            weigh(H0 - 1)
                            wait_apart(pe, begun, o_quant, g + 1)
                            for k in range(KC):
                                mm = pe.transpose(miscb[:, k * P:k * P + P], qo[:, k * P:k * P + P], c["identb"][:])
                            mm.then_inc(o_turned, 1)
                            wait_apart(pe, begun, o_copied, g + 1)
                            for k in range(KC):
                                mm = pe.matmul(misc[:], oT[:, k], woT[:, k], start=(k == 0), stop=(k == KC - 1))
                            mm.then_inc(projected, 1)

            @block.vector
            def _(dve):
                step = Chain(dve, step_dve)
                dve.sem_inc(tile_done, 2)
                with dve.Fori(0, B) as b:
                    step.restart()
                    dve.wait_ge(ctx_hi, b + 1)
                    dve.tensor_tensor(ctx_s[1][:], ctx_f[:], ctx_s[0][:].bitcast(F32), ALU.subtract).then_inc(ctx_lo, 1)
                    for j in range(KC):
                        dve.wait_ge(k_hi, b * KC + (j + 1))
                        dve.scalar_tensor_tensor(k_s[1][:, j], bank[j][:], bk[:, j:j + 1], k_s[0][:, j].bitcast(F32),
                                                 ALU.add, ALU.subtract).then_inc(k_lo, 1)
                    for l in range(NT):
                        dve.wait_ge(v_done, b * NT + (l + 1))
                        dve.tensor_tensor(v[:, l], bank[4 + l % 2][:], bv_row[:], ALU.add).then_inc(v_copied, 1)
                    dve.wait_ge(x_loaded, b * 16 + 16)
                    for t in range(NT):
                        layer_norm(dve, step, var_ready, rstd_ready, b * NT + t, x4[:, t], m, xn[:])
                        step(quantise(dve, step, xn[:], m, qx[:]))
                        dve.tensor_scalar(diag[:], c["ident"][:], m["s"][:], None, ALU.mult).then_inc(x_quant, 1)
                        dve.wait_ge(x_turned, b * NT + (t + 1))
                        dve.tensor_copy(sx_row[:, t * P:t * P + P], o_ps[:, 0:P]).then_inc(step_dve, 1)
                        step.n += 1
                        dve.tensor_copy(qxT[:, :, t * P:t * P + P],
                                        miscb[:, 0:D].rearrange("p (k n) -> p k n", k=KC)).then_inc(x_copied, 1)
                    dve.wait_ge(step_dve, step.n)
                    for j in range(KC):
                        dve.wait_ge(q_done, b * KC + (j + 1))
                        dve.tensor_tensor(q_f[:, j], bank[j][:], sx_row[:], ALU.mult).then_inc(step_dve, 1)
                    step.n += KC
                    dve.wait_ge(step_dve, step.n)
                    for j in range(KC):
                        step(dve.tensor_scalar(q_f[:, j], q_f[:, j], swq[:, j:j + 1], bqs[:, j:j + 1],
                                               ALU.mult, ALU.add))
                    dve.sem_inc(q_fp, 1)
                    dve.wait_ge(q_hi, b + 1)
                    dve.tensor_tensor(q_s[1][:], q_f[:], q_s[0][:].bitcast(F32), ALU.subtract).then_inc(q_lo, 1)
                    with dve.Fori(0, NT // 2) as tp:
                      for u in range(2):
                        t = tp * 2 + u
                        g = b * NT + tp * 2 + u
                        step.restart()
                        for h in range(H0 + 3):
                            if h < H0:
                                if h >= 4:
                                    dve.wait_ge(turned, h - 3)
                                dve.wait_ge(scored, h + 1)
                                dve.tensor_tensor_reduce(prob[:, h % 4], score[h % 4][:], mask_t[u][:], -1.0, 3.0e38, ALU.add, ALU.min,
                                                         nmax[:, h % 4:h % 4 + 1]).then_inc(shifted, 1)
                            k = h - 3
                            if k >= 0 and k % 2 == 0:
                                dve.wait_ge(turned, k + 1)
                                if k >= 2:
                                    dve.wait_ge(summed, k - 1)
                                dve.tensor_copy(probT[:, 0], probT_ps[0][:]).then_inc(copied_dve, 1)
                        dve.wait_ge(expd, H0)
                        step(dve.reciprocal(rinv[:], rsum[:]))
                        dve.wait_ge(summed, H0)
                        clear_all(dve, (scored, shifted, expd, turned, copied_dve, copied_act, summed))
                        step(dve.tensor_tensor(o[:].rearrange("p (h e) -> p h e", h=H0),
                                               o_ps[:].rearrange("p (h e) -> p h e", h=H0),
                                               rinv[:].rearrange("p (h e) -> p h e", e=1).to_broadcast([P, H0, D0]),
                                               ALU.mult))
                        quantise(dve, step, o[:], m, qo[:]).then_inc(o_quant, 1)
                        dve.wait_ge(o_turned, g + 1)
                        dve.tensor_copy(oT[:].rearrange("p k n -> p (k n)"), miscb[:, 0:D]).then_inc(o_copied, 1)
                        dve.wait_ge(projected, g + 1)
                        step(dve.tensor_tensor(o[:], misc[:], swo_row[:], ALU.mult))
                        step(dve.scalar_tensor_tensor(o[:], o[:], m["s"][:], bo_row[:], ALU.mult, ALU.add))
                        dve.scalar_tensor_tensor(x4[:, bass.ds(t, 1)], o[:].rearrange("p (a n) -> p a n", a=1), gate[:],
                                                 x4[:, bass.ds(t, 1)], ALU.mult, ALU.add).then_inc(tile_done, 1)
        st.clear()


def prepare_layer0_weights(nc, d, c, gate, wqT, woT, swq, bqs, bk, swo_row, bv_row, bo_row, wk, wv, bank):
    with ExitStack() as ctx:
        st = Stage(nc, ctx, "w0")
        sb, sem = st.sb, st.sem
        nat = [sb(f"nat{i}", [P, KC, D], F32) for i in range(2)]
        full = [sb(f"full{i}", [P, KC, D], F32) for i in range(2)]
        q_int = [sb(f"q_int{i}", [P, KC, D], BF16) for i in range(2)]
        tmp = sb("tmp", [P, KC, D], F32)
        bq = sb("bq", [P, KC], F32)
        amax, scale, inv = (sb(n, [P, 2, KC], F32) for n in ("amax", "scale", "inv"))
        diag = sb("diag", [P, KC, P], F32)
        loaded, made, rounded, turned, copied, spread, spread_out, split_hi, split_lo, step_dve, gated = (
            sem(n) for n in "loaded made rounded turned copied spread spread_out split_hi split_lo step_dve gated".split())
        LOADS = 9
        with nc.Block() as block:

            @block.sync
            def _(sp):
                for to, of in ((nat[0], "L0_wq"), (nat[1], "L0_wo"), (full[0], "L0_wkT"), (full[1], "L0_wvT")):
                    sp.dma_start(to[:], d[of].rearrange("(k p) n -> p k n", p=P)).then_inc(loaded, 16)
                sp.dma_start(bq[:], d["L0_bq"].rearrange("(p k) -> p k", p=P)).then_inc(loaded, 16)
                sp.dma_start(bk[:], d["L0_bk"].rearrange("(p k) -> p k", p=P)).then_inc(loaded, 16)
                sp.dma_start(bv_row[:], row_of(d["L0_bv"], 0, D)).then_inc(loaded, 16)
                sp.dma_start(bo_row[:], row_of(d["L0_bo"], 0, D)).then_inc(loaded, 16)
                sp.dma_start(gate[:], row_of(d["g_xattn"], 0, 1)).then_inc(loaded, 16)

            @block.gpsimd
            def _(pool):
                make_constants(pool, c, made)

            @block.scalar
            def _(act):
                act.wait_ge(loaded, 16 * LOADS)
                act.activation(gate[:], gate[:], ACT.Tanh).then_inc(gated, 1)
                act.activation(wk[0][:], full[0][:], ACT.Copy).then_inc(split_hi, 1)
                act.activation(wv[0][:], full[1][:], ACT.Copy).then_inc(split_hi, 1)

            @block.tensor
            def _(pe):
                pe.wait_ge(made, CONSTS)
                for w in range(2):
                    pe.wait_ge(rounded, w + 1)
                    for j in range(KC):
                        for k in range(KC):
                            mm = pe.transpose(bank[w * KC + j][:, :].bitcast(BF16)[:, k * P:k * P + P],
                                              q_int[w][:, j, k * P:k * P + P], c["identb"][:])
                        mm.then_inc(turned, 1)
                pe.wait_ge(spread, 1)
                pe.wait_ge(copied, 1)
                for j in range(KC):
                    mm = pe.matmul(bank[0][:, j * P:j * P + P], c["ones"][:], diag[:, j], start=True, stop=True)
                mm.then_inc(spread_out, 1)

            @block.vector
            def _(dve):
                step = Chain(dve, step_dve)
                dve.wait_ge(loaded, 16 * LOADS)
                for w in range(2):
                    step(dve.tensor_reduce(amax[:, w], nat[w][:], AX.X, ALU.max, apply_absolute_value=True))
                    step(dve.tensor_scalar(scale[:, w], amax[:, w], float(np.float32(1 / 127)), 1e-8, ALU.mult, ALU.max))
                    step(dve.reciprocal(inv[:, w], scale[:, w]))
                    for j in range(KC):
                        step(dve.tensor_scalar(tmp[:, j], nat[w][:, j], inv[:, w, j:j + 1], 127.0, ALU.mult, ALU.min))
                    step(dve.tensor_scalar(tmp[:], tmp[:], -127.0, ROUND, ALU.max, ALU.add))
                    dve.tensor_scalar(q_int[w][:], tmp[:], ROUND, None, ALU.subtract).then_inc(rounded, 1)
                dve.tensor_scalar(swq[:], scale[:, 0], SCALE0, None, ALU.mult)
                dve.tensor_scalar(bqs[:], bq[:], SCALE0, None, ALU.mult)
                dve.wait_ge(made, CONSTS)
                for j in range(KC):
                    ds = dve.tensor_scalar(diag[:, j], c["ident"][:], scale[:, 1, j:j + 1], None, ALU.mult)
                ds.then_inc(spread, 1)
                for w, to in enumerate((wqT, woT)):
                    for j in range(KC):
                        dve.wait_ge(turned, w * KC + j + 1)
                        dve.tensor_copy(to[:, :, j * P:j * P + P],
                                        bank[w * KC + j][:, :].bitcast(BF16)[:, 0:D].rearrange("p (k n) -> p k n", k=KC)
                                        ).then_inc(copied, 1)
                dve.wait_ge(spread_out, 1)
                dve.tensor_copy(swo_row[:], bank[0][:])
                for i, w in enumerate((wk, wv)):
                    dve.wait_ge(split_hi, i + 1)
                    dve.tensor_tensor(w[1][:], full[i][:], w[0][:].bitcast(F32), ALU.subtract).then_inc(split_lo, 1)
        st.clear()


I0 = 1408
IC = I0 // P
RMS_EPS = 1e-6
SUB = 2
UN = SUB * P


def dequantise_fp4(nc, d, gu, dn):
    with ExitStack() as ctx:
        st = Stage(nc, ctx, "f4")
        sb, sem = st.sb, st.sem
        work = []
        for g in range(KC):
            for o in range(0, 2 * I0, I0):
                work.append(("L0_guT", g * 16, o, "L0_gu_scales", g, I0, [w[:, g, o:o + I0] for w in gu]))
        for g in range(IC):
            work.append(("L0_dnT", g * 16, 0, "L0_dn_scales", g, D, [w[:, g, :] for w in dn]))
        words = [sb(f"words{i}", [P, I0], I32) for i in range(2)]
        scale = [sb(f"scale{i}", [P, I0], F16) for i in range(2)]
        code, sign = sb("code", [P, I0], I32), sb("sign", [P, I0], I32)
        over4, over6, size, half = (sb(n, [P, I0], BF16) for n in ("over4", "over6", "size", "half"))
        full = [sb(f"full{i}", [P, I0], F32) for i in range(2)]
        shift = sb("shift", [P, 1], I32)
        loaded = [sem("loaded0"), sem("loaded1")]
        shift_loaded, used, dequantised, split_hi, split_lo, step_dve = (
            sem(n) for n in "shift_loaded used dequantised split_hi split_lo step_dve".split())
        with nc.Block() as block:

            @block.sync
            def _(sp):
                sp.dma_start(shift[:], d["shifts"]).then_inc(shift_loaded, 16)
                for n, (src, r, col, ssrc, g, w, _to) in enumerate(work):
                    if n >= 2:
                        sp.wait_ge(used, n - 1)
                    a = d[src]
                    wide = a.shape[1]
                    sp.dma_start(words[n % 2][:, 0:w], bass.AP(
                        tensor=a.tensor, offset=a.offset + r * wide + col, ap=[[wide, 16], [0, 8], [1, w]]
                    )).then_inc(loaded[n % 2], 16)
                    s = d[ssrc]
                    sp.dma_start(scale[n % 2][:, 0:w], row_of(s, g * s.shape[1] + col, w)).then_inc(loaded[n % 2], 16)

            @block.scalar
            def _(act):
                for n, (*_, w, to) in enumerate(work):
                    act.wait_ge(dequantised, n + 1)
                    act.activation(to[0], full[n % 2][:, 0:w], ACT.Copy).then_inc(split_hi, 1)

            @block.vector
            def _(dve):
                step = Chain(dve, step_dve)
                dve.wait_ge(shift_loaded, 16)

                def low_part(n):
                    w, to = work[n][5:]
                    dve.wait_ge(split_hi, n + 1)
                    dve.tensor_tensor(to[1], full[n % 2][:, 0:w], to[0].bitcast(F32), ALU.subtract).then_inc(split_lo, 1)

                for n, (*_, w, to) in enumerate(work):
                    dve.wait_ge(loaded[n % 2], 32 * (n // 2 + 1))
                    wd = words[n % 2][:, 0:w]
                    step(dve.tensor_scalar(code[:, 0:w], wd, shift[:], 7, ALU.logical_shift_right, ALU.bitwise_and))
                    step(dve.tensor_scalar(sign[:, 0:w], wd, shift[:], 8, ALU.logical_shift_right, ALU.bitwise_and))
                    dve.tensor_scalar(over4[:, 0:w], code[:, 0:w], 4.0, 0.0, ALU.subtract, ALU.max).then_inc(step_dve, 1)
                    dve.tensor_scalar(over6[:, 0:w], code[:, 0:w], 6.0, 0.0, ALU.subtract, ALU.max).then_inc(step_dve, 1)
                    step.n += 2
                    dve.wait_ge(step_dve, step.n)
                    step(dve.scalar_tensor_tensor(size[:, 0:w], over6[:, 0:w], 2.0, over4[:, 0:w], ALU.mult, ALU.add))
                    step(dve.tensor_tensor(size[:, 0:w], size[:, 0:w], code[:, 0:w], ALU.add))
                    step(dve.tensor_scalar(half[:, 0:w], sign[:, 0:w], -0.125, 0.5, ALU.mult, ALU.add))
                    step(dve.tensor_tensor(size[:, 0:w], size[:, 0:w], half[:, 0:w], ALU.mult))
                    if n >= 2:
                        dve.wait_ge(split_lo, n - 1)
                    step(dve.tensor_tensor(full[n % 2][:, 0:w], size[:, 0:w], scale[n % 2][:, 0:w], ALU.mult))
                    dve.sem_inc(dequantised, 1)
                    dve.sem_inc(used, 1)
                    if n:
                        low_part(n - 1)
                low_part(len(work) - 1)
        st.clear()


def layer0_ffn(nc, d, x_in, x_out):
    with ExitStack() as ctx:
        st = Stage(nc, ctx, "f0")
        sb, ps, sem = st.sb, st.ps, st.sem
        gu = [sb(f"gu{i}", [P, KC, 2 * I0], F32R) for i in range(2)]
        dn = [sb(f"dn{i}", [P, IC, D], F32R) for i in range(2)]
        dequantise_fp4(nc, d, gu, dn)
        c = constants(st, nc)
        gate = sb("gate", [P, 1], F32)
        m = norm_buffers(st)
        x = [sb(f"x{i}", [P, SUB, D], F32) for i in range(2)]
        xn = sb("xn", [P, SUB, D], F32)
        xT = [sb(f"xT{i}", [P, KC, UN], F32R) for i in range(2)]
        th = sb("th", [P, 2, UN], F32)
        hf = sb("hf", [P, 2, UN], F32)
        hT = [sb(f"hT{i}", [P, IC, UN], F32R) for i in range(2)]
        sq = sb("sq", [P, D], F32)
        ss = sb("ss", [P, 1], F32)
        ms = sb("ms", [P, 1], F32)
        rr = sb("rr", [P, 1], F32)
        rg = sb("rg", [P, 1], F32)
        bank = [ps(f"bank{i}", [P, 512], F32) for i in range(8)]
        gu_ps, xT_ps, y_ps = bank[0:4], bank[4:6], bank[6:8]
        (consts_made, gate_loaded, gated, round_done, x_ready, normed, x_turned, x_hi, x_lo, gu_done, tanhed,
         h_made, h_hi, h_lo, y_done, squared, var_ready, rstd_ready, ms_ready, rms_ready, y_used, step_dve, passed_sp) = (
             sem(n) for n in "consts_made gate_loaded gated round_done x_ready normed x_turned x_hi x_lo gu_done "
             "tanhed h_made h_hi h_lo y_done squared var_ready rstd_ready ms_ready rms_ready y_used step_dve passed_sp".split())
        loaded = [sem("loaded0"), sem("loaded1")]
        stored = [sem("stored0"), sem("stored1")]
        of_round = (normed, x_turned, x_hi, x_lo, gu_done, tanhed, h_made, h_hi, h_lo, y_done, squared,
                    var_ready, rstd_ready, ms_ready, rms_ready, y_used)
        x_src = x_in.rearrange("(n t p) d -> n p t d", p=P, t=SUB)
        x_dst = x_out.rearrange("(n t p) d -> n p t d", p=P, t=SUB)
        ROUNDS = TILES // SUB // 2

        with nc.Block() as block:

            @block.sync
            def _(sp):
                sp.dma_start(gate[:], row_of(d["g_ffn"], 0, 1)).then_inc(gate_loaded, 16)
                with sp.Fori(0, ROUNDS) as n:
                    for u in range(2):
                        sp.dma_start(x[u][:], x_src[n * 2 + u]).then_inc(loaded[u], 16)
                    for u in range(2):
                        sp.wait_ge(x_ready, n * 2 + (u + 1))
                        sp.dma_start(x_dst[n * 2 + u], x[u][:]).then_inc(stored[u], 16)
                    for u in range(2):
                        pass_wait(sp, passed_sp, stored[u], n * 16 + 16)

            @block.gpsimd
            def _(pool):
                make_constants(pool, c, consts_made)
                with pool.Fori(0, ROUNDS) as n:
                    def root(of, to, ready, done, k):
                        pool.wait_ge(ready, k)
                        pool.tensor_tensor(to[:], of[:], c["mhalf"][:], ALU.pow).then_inc(done, 1)
                    for k in range(2 * SUB):
                        root(m["ve"], m["rstd"], var_ready, rstd_ready, k + 1)
                    for k in range(2 * SUB):
                        root(ms, rr, ms_ready, rms_ready, k + 1)
                    pool.wait_ge(round_done, n + 1)

            @block.scalar
            def _(act):
                act.wait_ge(gate_loaded, 16)
                act.activation(gate[:], gate[:], ACT.Tanh).then_inc(gated, 1)
                with act.Fori(0, ROUNDS) as n:
                    def context(u):
                        for t in range(SUB):
                            act.wait_ge(x_turned, u * SUB + t + 1)
                            act.activation(xT[0][:, :, t * P:t * P + P],
                                           xT_ps[t][:].rearrange("p (k n) -> p k n", k=KC), ACT.Copy).then_inc(x_hi, 1)

                    def inner(u):
                        for i in range(IC + 1):
                            if i < IC:
                                k = u * IC + i
                                act.wait_ge(gu_done, k + 1)
                                if k >= 2:
                                    act.wait_ge(h_made, k - 1)
                                act.activation(th[:, k % 2], gu_ps[k % 4][:, 0:UN], ACT.Tanh, scale=0.5).then_inc(tanhed, 1)
                            if i:
                                k = u * IC + i - 1
                                act.wait_ge(h_made, k + 1)
                                act.activation(hT[0][:, i - 1], hf[:, k % 2], ACT.Copy).then_inc(h_hi, 1)

                    def square(u):
                        for t in range(SUB):
                            k = u * SUB + t
                            act.wait_ge(y_done, k + 1)
                            if k:
                                act.wait_ge(ms_ready, k)
                            act.activation(sq[:], y_ps[t][:], ACT.Square, accum_out=ss[:]).then_inc(squared, 1)

                    context(0)
                    inner(0)
                    context(1)
                    square(0)
                    inner(1)
                    square(1)
                    act.wait_ge(round_done, n + 1)

            @block.tensor
            def _(pe):
                pe.wait_ge(consts_made, CONSTS)
                with pe.Fori(0, ROUNDS) as n:
                    def turn(u):
                        for t in range(SUB):
                            pe.wait_ge(normed, u * SUB + t + 1)
                            for k in range(KC):
                                mm = pe.transpose(xT_ps[t][:, k * P:k * P + P], xn[:, t, k * P:k * P + P], c["ident"][:])
                            mm.then_inc(x_turned, 1)

                    def up(u):
                        pe.wait_ge(x_hi, u * SUB + SUB)
                        pe.wait_ge(x_lo, u * SUB + SUB)
                        for i in range(IC):
                            j = u * IC + i
                            if j >= 4:
                                pe.wait_ge(h_made, j - 3)
                            for half in range(2):
                                o = half * I0 + i * P
                                for k in range(KC):
                                    mm = mm3(pe, gu_ps[j % 4][:, half * UN:half * UN + UN],
                                             [w[:, k, o:o + P] for w in gu], [a[:, k] for a in xT],
                                             k == 0, k == KC - 1)
                            mm.then_inc(gu_done, 1)

                    def down(u):
                        pe.wait_ge(h_hi, u * IC + IC)
                        pe.wait_ge(h_lo, u * IC + IC)
                        for t in range(SUB):
                            if u:
                                pe.wait_ge(y_used, t + 1)
                            for i in range(IC):
                                mm = mm3(pe, y_ps[t][:], [a[:, i, t * P:t * P + P] for a in hT],
                                         [w[:, i] for w in dn], i == 0, i == IC - 1)
                            mm.then_inc(y_done, 1)

                    turn(0)
                    up(0)
                    turn(1)
                    down(0)
                    up(1)
                    down(1)
                    pe.wait_ge(round_done, n + 1)

            @block.vector
            def _(dve):
                step = Chain(dve, step_dve)
                dve.wait_ge(gated, 1)
                with dve.Fori(0, ROUNDS) as n:
                    step.restart()

                    def norm(u):
                        for t in range(SUB):
                            if u:
                                dve.wait_ge(x_turned, t + 1)
                            layer_norm(dve, step, var_ready, rstd_ready, u * SUB + t, x[u][:, t], m, xn[:, t])
                            dve.sem_inc(normed, 1)

                    def context(u):
                        for t in range(SUB):
                            dve.wait_ge(x_hi, u * SUB + t + 1)
                            part = [a[:, :, t * P:t * P + P] for a in xT]
                            dve.tensor_tensor(part[1], xT_ps[t][:].rearrange("p (k n) -> p k n", k=KC),
                                              part[0].bitcast(F32), ALU.subtract).then_inc(x_lo, 1)

                    def inner(u):
                        for i in range(IC + 1):
                            if i < IC:
                                k = u * IC + i
                                dve.wait_ge(tanhed, k + 1)
                                if k >= 2:
                                    dve.wait_ge(h_lo, k - 1)
                                step(dve.scalar_tensor_tensor(hf[:, k % 2], th[:, k % 2], 1.0, gu_ps[k % 4][:, 0:UN],
                                                              ALU.add, ALU.mult))
                                dve.scalar_tensor_tensor(hf[:, k % 2], hf[:, k % 2], 0.5, gu_ps[k % 4][:, UN:2 * UN],
                                                         ALU.mult, ALU.mult).then_inc(h_made, 1)
                            if i:
                                k = u * IC + i - 1
                                dve.wait_ge(h_hi, k + 1)
                                dve.tensor_tensor(hT[1][:, i - 1], hf[:, k % 2], hT[0][:, i - 1].bitcast(F32),
                                                  ALU.subtract).then_inc(h_lo, 1)

                    def add(u):
                        for t in range(SUB):
                            k = u * SUB + t
                            dve.wait_ge(squared, k + 1)
                            dve.tensor_scalar(ms[:], ss[:], 1.0 / D, RMS_EPS, ALU.mult, ALU.add).then_inc(ms_ready, 1)
                            dve.wait_ge(rms_ready, k + 1)
                            step(dve.tensor_tensor(rg[:], rr[:], gate[:], ALU.mult))
                            step(dve.scalar_tensor_tensor(x[u][:, t], y_ps[t][:], rg[:], x[u][:, t], ALU.mult, ALU.add))
                            dve.sem_inc(y_used, 1)
                        dve.sem_inc(x_ready, 1)

                    dve.wait_ge(loaded[0], n * 16 + 16)
                    norm(0)
                    context(0)
                    dve.wait_ge(loaded[1], n * 16 + 16)
                    norm(1)
                    inner(0)
                    context(1)
                    add(0)
                    inner(1)
                    add(1)
                    clear_all(dve, of_round)
                    dve.sem_inc(round_done, 1)
        st.clear()


H1 = 16
G1 = 4
HD = 128
CTX = S
M1 = CTX + S
QK_EPS = 1e-6
SCALE1 = float(1.0 / np.sqrt(HD))
Q_CHUNKS = H1 * HD // 512
K_SELF, V_SELF, K_CTX, V_CTX = Q_CHUNKS, Q_CHUNKS + 1, Q_CHUNKS + 2, Q_CHUNKS + 3
CHUNKS = Q_CHUNKS + 4
TURNED = Q_CHUNKS + 2


def layer1_projections(nc, d, x_in, scr):
    with ExitStack() as ctx:
        st = Stage(nc, ctx, "p1")
        sb, ps, sem = st.sb, st.ps, st.sem
        c = constants(st, nc)
        w = [sb(f"w{i}", [P, CHUNKS, KC, 512], F32R) for i in range(2)]
        cosw, sinw = (sb(n, [P, 2, NT, HD], F32) for n in ("cosw", "sinw"))
        kw = sb("kw", [P, HD], F32)
        split_layer1_weights(nc, d, w, cosw, sinw, kw)

        m = norm_buffers(st)
        x = sb("x", [P, D], F32)
        cx = sb("cx", [P, KC, P], F32)
        xn = sb("xn", [P, D], F32)
        xT = [sb(f"xT{i}", [P, KC, P], F32R) for i in range(2)]
        cT = [sb(f"cT{i}", [P, KC, P], F32R) for i in range(2)]
        sq = sb("sq", [P, 512], F32)
        ss, ms, rr = (sb(n, [P, TURNED, 4], F32) for n in ("ss", "ms", "rr"))
        r_out = sb("r_out", [P, Q_CHUNKS, 4], F32)
        seed = sb("seed", [P, 1], F32)
        mhalf4 = sb("mhalf4", [P, 4], F32)
        rot, cosed = sb("rot", [P, 2, 512], F32), sb("cosed", [P, 2, 512], F32)
        roped = sb("roped", [P, 2, 512], F32)
        turned = [sb(f"turned{i}", [P, TURNED, 512], F32R) for i in range(2)]
        vs = [sb(f"vs{i}", [P, 2, 512], F32R) for i in range(2)]
        bank = [ps(f"bank{i}", [P, 512], F32) for i in range(8)]
        pr_ps, t_ps, x_ps = bank[0:4], bank[4:6], bank[6]
        names = ("consts_made round_done normed x_turned x_hi x_lo c_hi c_lo produced squared summed_sq ms_ready rms_ready "
                 "rotated added scaled turned_ps t_hi t_lo v_hi v_lo var_ready rstd_ready chunk_free "
                 "x_loaded c_loaded in_used out_ready stored step_dve passed_sp passed_act")
        s = {n: sem(n) for n in names.split()}
        of_round = [s[n] for n in ("normed x_turned x_hi x_lo c_hi c_lo produced squared summed_sq ms_ready rms_ready "
                                   "rotated added scaled turned_ps t_hi t_lo v_hi v_lo var_ready rstd_ready chunk_free").split()]
        x_src = x_in.rearrange("(g p) d -> g p d", p=P)
        ctxT_src = d["ctxT"].rearrange("b (k p) (t s) -> b t p k s", p=P, s=P)
        order = list(range(CHUNKS))
        rope_chunks = list(range(Q_CHUNKS + 1))

        with nc.Block() as block:

            @block.sync
            def _(sp):
                with sp.Fori(0, B) as b:
                    with sp.Fori(0, NT) as t:
                        g = b * NT + t
                        pass_wait(sp, s["passed_sp"], s["in_used"], g + 1)
                        sp.dma_start(x[:], x_src[g]).then_inc(s["x_loaded"], 16)
                        sp.dma_start(cx[:], ctxT_src[b, t]).then_inc(s["c_loaded"], 16)

            @block.gpsimd
            def _(pool):
                make_constants(pool, c, s["consts_made"])
                pool.memset(mhalf4[:], -0.5).then_inc(s["consts_made"], 1)
                pool.wait_ge(s["consts_made"], CONSTS + 1)
                with pool.Fori(0, B) as b:
                    with pool.Fori(0, NT) as t:
                        pool.wait_ge(s["var_ready"], 1)
                        pool.tensor_tensor(m["rstd"][:], m["ve"][:], c["mhalf"][:], ALU.pow).then_inc(s["rstd_ready"], 1)
                        for n, ch in enumerate(rope_chunks + [TURNED - 1]):
                            pool.wait_ge(s["ms_ready"], n + 1)
                            pool.tensor_tensor(rr[:, ch], ms[:, ch], mhalf4[:], ALU.pow).then_inc(s["rms_ready"], 1)
                            if ch in rope_chunks:
                                pool.wait_ge(s["rotated"], n + 1)
                                if n >= 2:
                                    pool.wait_ge(s["turned_ps"], n - 1)
                                pool.tensor_tensor(roped[:, n % 2], cosed[:, n % 2], rot[:, n % 2], ALU.add).then_inc(s["added"], 1)
                        pool.wait_ge(s["round_done"], b * NT + t + 2)

            @block.scalar
            def _(act):
                act.dma_start(seed[:], row_of(d["L1_q_norm"], 0, 1)).then_inc(s["stored"], 16)
                with act.Fori(0, B) as b:
                    with act.Fori(0, NT) as t:
                        act.wait_ge(s["c_loaded"], (b * NT + t) * 16 + 16)
                        act.activation(cT[0][:], cx[:], ACT.Copy).then_inc(s["c_hi"], 1)
                        act.wait_ge(s["x_turned"], 1)
                        act.activation(xT[0][:].rearrange("p k n -> p (k n)"), x_ps[:], ACT.Copy).then_inc(s["x_hi"], 1)

                        def turn_hi(n):
                            act.wait_ge(s["turned_ps"], n + 1)
                            act.activation(turned[0][:, n], t_ps[n % 2][:], ACT.Copy).then_inc(s["t_hi"], 1)
                        n_t = n_v = 0
                        for n, ch in enumerate(order):
                            act.wait_ge(s["produced"], n + 1)
                            if ch in (V_SELF, V_CTX):
                                act.activation(vs[0][:, n_v], pr_ps[n % 4][:], ACT.Copy).then_inc(s["v_hi"], 1)
                                n_v += 1
                            else:
                                if n_t:
                                    act.wait_ge(s["summed_sq"], n_t)
                                act.activation(sq[:], pr_ps[n % 4][:], ACT.Square).then_inc(s["squared"], 1)
                                n_t += 1
                                if n_t == 3:
                                    pass_wait(act, s["passed_act"], s["stored"], (b * NT + t) * (11 * 16) + 16)
                                if n_t >= 3:
                                    turn_hi(n_t - 3)
                        turn_hi(TURNED - 2)
                        turn_hi(TURNED - 1)
                        pass_wait(act, s["passed_act"], s["out_ready"], b * NT + t + 1)
                        for i in range(2):
                            def put(to, of):
                                act.dma_start(to, of.bitcast(F32)).then_inc(s["stored"], 16)
                            put(scr["q"][i][b, t], turned[i][:, 0:Q_CHUNKS])
                            put(scr["k"][i][b][:, :, bass.ds(t * P + CTX, P)],
                                turned[i][:, K_SELF].rearrange("p (g n) -> p g n", g=G1))
                            put(scr["k"][i][b][:, :, bass.ds(t * P, P)],
                                turned[i][:, TURNED - 1].rearrange("p (g n) -> p g n", g=G1))
                            put(scr["v"][i][b][:, bass.ds(t + NT, 1)], vs[i][:, 0:1])
                            put(scr["v"][i][b][:, bass.ds(t, 1)], vs[i][:, 1:2])
                        act.dma_start(scr["r"][b, t], r_out[:]).then_inc(s["stored"], 16)
                        pass_wait(act, s["passed_act"], s["round_done"], b * NT + t + 2)
                act.wait_ge(s["stored"], TILES * (11 * 16) + 16)

            @block.tensor
            def _(pe):
                pe.wait_ge(s["consts_made"], CONSTS)
                with pe.Fori(0, B) as b:
                    with pe.Fori(0, NT) as t:
                        pe.wait_ge(s["normed"], 1)
                        for k in range(KC):
                            mm = pe.transpose(x_ps[:, k * P:k * P + P], xn[:, k * P:k * P + P], c["ident"][:])
                        mm.then_inc(s["x_turned"], 1)

                        def turn(n):
                            if n < Q_CHUNKS:
                                pe.wait_ge(s["added"], n + 1)
                            else:
                                pe.wait_ge(s["scaled"], n - Q_CHUNKS + 1)
                            if n >= 2:
                                pe.wait_ge(s["t_lo"], n - 1)
                            for k in range(4):
                                mm = pe.transpose(t_ps[n % 2][:, k * P:k * P + P], roped[:, n % 2, k * P:k * P + P], c["ident"][:])
                            mm.then_inc(s["turned_ps"], 1)
                        n_t = 0
                        for n, ch in enumerate(order):
                            if n == 0:
                                pe.wait_ge(s["x_hi"], 1)
                                pe.wait_ge(s["x_lo"], 1)
                            if ch == K_CTX:
                                pe.wait_ge(s["c_hi"], 1)
                                pe.wait_ge(s["c_lo"], 1)
                            if n >= 4:
                                pe.wait_ge(s["chunk_free"], n - 3)
                            of = cT if ch in (K_CTX, V_CTX) else xT
                            for k in range(KC):
                                mm = mm3(pe, pr_ps[n % 4][:], [a[:, k] for a in of], [a[:, ch, k] for a in w],
                                         k == 0, k == KC - 1)
                            mm.then_inc(s["produced"], 1)
                            if n >= 2 and n_t < TURNED:
                                if n_t < Q_CHUNKS or n >= 6:
                                    turn(n_t)
                                    n_t += 1
                        while n_t < TURNED:
                            turn(n_t)
                            n_t += 1
                        pe.wait_ge(s["round_done"], b * NT + t + 2)

            @block.vector
            def _(dve):
                step = Chain(dve, s["step_dve"])
                dve.sem_inc(s["round_done"], 1)
                dve.sem_inc(s["in_used"], 1)
                with dve.Fori(0, B) as b:
                    with dve.Fori(0, NT) as t:
                        step.restart()
                        dve.wait_ge(s["x_loaded"], (b * NT + t) * 16 + 16)
                        layer_norm(dve, step, s["var_ready"], s["rstd_ready"], 0, x[:], m, xn[:])
                        dve.sem_inc(s["normed"], 1)
                        dve.wait_ge(s["c_hi"], 1)
                        dve.tensor_tensor(cT[1][:], cx[:], cT[0][:].bitcast(F32), ALU.subtract).then_inc(s["c_lo"], 1)
                        dve.wait_ge(s["c_lo"], 1)
                        dve.sem_inc(s["in_used"], 1)
                        dve.wait_ge(s["x_hi"], 1)
                        dve.tensor_tensor(xT[1][:].rearrange("p k n -> p (k n)"), x_ps[:],
                                          xT[0][:].rearrange("p k n -> p (k n)").bitcast(F32), ALU.subtract).then_inc(s["x_lo"], 1)

                        def turn_lo(n):
                            dve.wait_ge(s["t_hi"], n + 1)
                            dve.tensor_tensor(turned[1][:, n], t_ps[n % 2][:], turned[0][:, n].bitcast(F32),
                                              ALU.subtract).then_inc(s["t_lo"], 1)
                        n_t = n_v = 0
                        for n, ch in enumerate(order):
                            dve.wait_ge(s["produced"], n + 1)
                            src = pr_ps[n % 4][:]
                            if ch in (V_SELF, V_CTX):
                                dve.wait_ge(s["v_hi"], n_v + 1)
                                dve.tensor_tensor(vs[1][:, n_v], src, vs[0][:, n_v].bitcast(F32), ALU.subtract).then_inc(s["v_lo"], 1)
                                n_v += 1
                                dve.wait_ge(s["v_lo"], n_v)
                                dve.sem_inc(s["chunk_free"], 1)
                                continue
                            dve.wait_ge(s["squared"], n_t + 1)
                            dve.tensor_reduce(ss[:, n_t], sq[:].rearrange("p (h e) -> p h e", h=4), AX.X, ALU.add).then_inc(s["summed_sq"], 1)
                            dve.wait_ge(s["summed_sq"], n_t + 1)
                            dve.tensor_scalar(ms[:, n_t], ss[:, n_t], 1.0 / HD, QK_EPS, ALU.mult, ALU.add).then_inc(s["ms_ready"], 1)
                            src4 = src.rearrange("p (h e) -> p h e", h=4)
                            r = rr[:, n_t].rearrange("p (h e) -> p h e", e=1).to_broadcast([P, 4, HD])
                            rop = roped[:, n_t % 2].rearrange("p (h e) -> p h e", h=4)
                            if ch in rope_chunks:
                                which = 0 if ch < Q_CHUNKS else 1
                                half = HD // 2
                                rt = rot[:, n_t % 2].rearrange("p (h e) -> p h e", h=4)
                                cs = cosed[:, n_t % 2].rearrange("p (h e) -> p h e", h=4)
                                if n_t >= 2:
                                    dve.wait_ge(s["added"], n_t - 1)

                                def over_heads(a):
                                    return a.to_broadcast([P, 4, a.shape[2]])
                                dve.tensor_tensor(cs, src4, over_heads(cosw[:, which, bass.ds(t, 1)]), ALU.mult)
                                dve.tensor_tensor(rt[:, :, 0:half], src4[:, :, half:], over_heads(sinw[:, which, bass.ds(t, 1), 0:half]), ALU.mult)
                                step(dve.tensor_tensor(rt[:, :, half:], src4[:, :, 0:half], over_heads(sinw[:, which, bass.ds(t, 1), half:]), ALU.mult))
                                dve.sem_inc(s["rotated"], 1)
                                dve.sem_inc(s["chunk_free"], 1)
                                if ch == K_SELF:
                                    dve.wait_ge(s["added"], n_t + 1)
                                    dve.wait_ge(s["rms_ready"], n_t + 1)
                                    dve.tensor_tensor(rop, rop, r, ALU.mult).then_inc(s["scaled"], 1)
                            else:
                                if n_t >= 2:
                                    dve.wait_ge(s["turned_ps"], n_t - 1)
                                step(dve.tensor_tensor(rop, src4, kw[:].rearrange("p (h e) -> p h e", h=1).to_broadcast([P, 4, HD]), ALU.mult))
                                dve.sem_inc(s["chunk_free"], 1)
                                dve.wait_ge(s["rms_ready"], n_t + 1)
                                dve.tensor_tensor(rop, rop, r, ALU.mult).then_inc(s["scaled"], 1)
                            n_t += 1
                            if n_t >= 4:
                                turn_lo(n_t - 4)
                        for n in range(TURNED - 3, TURNED):
                            turn_lo(n)
                        dve.wait_ge(s["t_lo"], TURNED)
                        step(dve.tensor_copy(r_out[:], rr[:, 0:Q_CHUNKS]))
                        clear_all(dve, of_round)
                        dve.sem_inc(s["out_ready"], 1)
                        dve.sem_inc(s["round_done"], 1)
        st.clear()


def split_layer1_weights(nc, d, w, cosw, sinw, kw):
    with ExitStack() as ctx:
        st = Stage(nc, ctx, "w1")
        sb, sem = st.sb, st.sem
        full = [sb(f"full{i}", [P, KC, 512], F32) for i in range(2)]
        nw = sb("nw", [P, 2, HD], F32)
        nwr = sb("nwr", [P, 2, HD], F32)
        cos, sin = sb("cos", [P, NT, HD], F32), sb("sin", [P, NT, HD], F32)
        loaded = [sem("loaded0"), sem("loaded1")]
        tables_loaded, split_hi, split_lo = (sem(n) for n in "tables_loaded split_hi split_lo".split())
        src = [(d["L1_wq"], q * 512) for q in range(Q_CHUNKS)] + [
            (d[n], 0) for n in ("L1_wk", "L1_wv", "L1_wk_ctx", "L1_wv_ctx")]
        with nc.Block() as block:

            @block.sync
            def _(sp):
                for to, of in ((cos, "cos"), (sin, "sin")):
                    sp.dma_start(to[:], d[of].rearrange("(t p) n -> p t n", p=P)).then_inc(tables_loaded, 16)
                for i, n in enumerate(("L1_q_norm", "L1_k_norm")):
                    sp.dma_start(nw[:, i], row_of(d[n], 0, HD)).then_inc(tables_loaded, 16)
                    half = HD // 2
                    sp.dma_start(nwr[:, i, 0:half], row_of(d[n], half, half)).then_inc(tables_loaded, 16)
                    sp.dma_start(nwr[:, i, half:], row_of(d[n], 0, half)).then_inc(tables_loaded, 16)
                for n, (a, col) in enumerate(src):
                    if n >= 2:
                        sp.wait_ge(split_lo, n - 1)
                    sp.dma_start(full[n % 2][:], a.rearrange("(k p) n -> p k n", p=P)[:, :, col:col + 512]).then_inc(loaded[n % 2], 16)

            @block.scalar
            def _(act):
                for n in range(CHUNKS):
                    act.wait_ge(loaded[n % 2], 16 * (n // 2 + 1))
                    act.activation(w[0][:, n], full[n % 2][:], ACT.Copy).then_inc(split_hi, 1)

            @block.vector
            def _(dve):
                dve.wait_ge(tables_loaded, 8 * 16)
                dve.tensor_copy(kw[:], nw[:, 1])
                for i in range(2):
                    for table, by, to in ((cos, nw, cosw), (sin, nwr, sinw)):
                        dve.tensor_tensor(to[:, i], table[:], by[:, i:i + 1].to_broadcast([P, NT, HD]), ALU.mult)
                for n in range(CHUNKS):
                    dve.wait_ge(split_hi, n + 1)
                    dve.tensor_tensor(w[1][:, n], full[n % 2][:], w[0][:, n].bitcast(F32), ALU.subtract).then_inc(split_lo, 1)
        st.clear()


def layer1_scratch(nc):
    def pair(name, shape):
        return [nc.dram_tensor(f"{name}_{p}", shape, F32, kind="Internal").ap() for p in ("hi", "lo")]
    return {"q": pair("l1_q", (B, NT, P, Q_CHUNKS, 512)), "k": pair("l1_k", (B, P, G1, M1)),
            "v": pair("l1_v", (B, P, M1 // P, 512)),
            "r": nc.dram_tensor("l1_r", (B, NT, P, Q_CHUNKS, 4), F32, kind="Internal").ap()}


BIG = -1e30


def layer1_attention(nc, d, x_in, scr, x_out):
    with ExitStack() as ctx:
        st = Stage(nc, ctx, "a1")
        sb, ps, sem = st.sb, st.ps, st.sem
        c = constants(st, nc)
        gate = sb("gate", [P, 1], F32)
        future = sb("future", [P, P], BF16)
        wo = [sb(f"wo{i}", [P, H1, D], F32R) for i in range(2)]
        split_output_weight(nc, d, c, wo, future, gate)

        kT = [sb(f"kT{i}", [P, G1, M1], F32R) for i in range(2)]
        v = [sb(f"v{i}", [P, M1 // P, 512], F32R) for i in range(2)]
        qT = [[sb(f"qT{u}{i}", [P, H1, P], F32R) for i in range(2)] for u in range(2)]
        r = sb("r", [P, 2, H1], F32)
        rs = sb("rs", [P, 2, H1], F32)
        x = sb("x", [P, 2, D], F32)
        prob = sb("prob", [P, 2, M1], F32)
        probT = [sb(f"probT{i}", [P, 2, M1], F32R) for i in range(2)]
        mx, nb = sb("mx", [P, 2], F32), sb("nb", [P, 2], F32)
        rsum, rinv = sb("rsum", [P, H1], F32), sb("rinv", [P, H1], F32)
        o = sb("o", [P, H1 * HD], F32)
        s_ps = ps("s_ps", [P, 2, M1], F32)
        t_ps = ps("t_ps", [P, M1], F32)
        o_ps = ps("o_ps", [P, 2, 512], F32)
        oT = [a.rearrange("p a m -> p (a m)") for a in (probT[0][:], probT[1][:])]
        names = ("scored maxed expd turned t_hi t_lo summed o_out scaled o_turned oT_hi oT_lo projected added "
                 "k_loaded v_loaded round_done begun stored x_ready step_dve")
        s = {n: sem(n) for n in names.split()}
        q_loaded = [sem("q_loaded0"), sem("q_loaded1")]
        of_round = [s[n] for n in "scored maxed expd turned t_hi t_lo summed o_out scaled projected added".split()]
        x_src = x_in.rearrange("(g p) d -> g p d", p=P)
        x_dst = x_out[0:T].rearrange("(g p) d -> g p d", p=P)
        HEADS = NT * H1

        steps = []
        for t in range(NT):
            steps += [("head", t, h) for h in range(H1)] + [("o", t, 0), ("o", t, 1)]
        heads = [k for k, (kind, *_ ) in enumerate(steps) if kind == "head"]
        head_no = {k: n for n, k in enumerate(heads)}

        def width(t):
            return CTX + (t + 1) * P

        with nc.Block() as block:

            @block.sync
            def _(sp):
                sp.sem_inc(s["begun"], 1)
                with sp.Fori(0, B) as b:
                    wait_apart(sp, s["begun"], s["round_done"], b + 1)
                    for i in range(2):
                        sp.dma_start(kT[i][:].bitcast(F32), scr["k"][i][b]).then_inc(s["k_loaded"], 16)

                    def load_q(t):
                        u = t % 2
                        for i in range(2):
                            sp.dma_start(qT[u][i][:].rearrange("p (c h) n -> p c (h n)", h=4).bitcast(F32),
                                         scr["q"][i][b, t]).then_inc(q_loaded[u], 16)
                        sp.dma_start(r[:, u].rearrange("p (c h) -> p c h", h=4), scr["r"][b, t]).then_inc(q_loaded[u], 16)
                        sp.dma_start(x[:, u], x_src[b * NT + t]).then_inc(q_loaded[u], 16)
                    load_q(0)
                    for i in range(2):
                        sp.dma_start(v[i][:].bitcast(F32), scr["v"][i][b]).then_inc(s["v_loaded"], 16)
                    load_q(1)
                    for t in range(NT):
                        wait_apart(sp, s["begun"], s["x_ready"], b * NT + (t + 1))
                        sp.dma_start(x_dst[b * NT + t], x[:, t % 2]).then_inc(s["stored"], 16)
                        if t + 2 < NT:
                            wait_apart(sp, s["begun"], s["stored"], b * (NT * 16) + (t + 1) * 16)
                            load_q(t + 2)

            @block.gpsimd
            def _(pool):
                pass

            @block.scalar
            def _(act):
                with act.Fori(0, B) as b:
                    def exp(k):
                        _, t, h = steps[k]
                        n = head_no[k]
                        w = width(t)
                        act.wait_ge(s["maxed"], n + 1)
                        if n >= 2:
                            act.wait_ge(s["turned"], heads[n - 2] + 1)
                        act.activation(prob[:, n % 2, 0:w], s_ps[:, n % 2, 0:w], ACT.Exp, bias=nb[:, n % 2:n % 2 + 1],
                                       scale=rs[:, t % 2, h:h + 1], accum_out=rsum[:, h:h + 1]).then_inc(s["expd"], 1)

                    def hi(k):
                        kind, t, _ = steps[k]
                        w = width(t) if kind == "head" else M1
                        act.wait_ge(s["turned"], k + 1)
                        if k >= 2:
                            act.wait_ge(s["summed"], k - 1)
                        act.activation(probT[0][:, k % 2, 0:w], t_ps[:, 0:w], ACT.Copy).then_inc(s["t_hi"], 1)

                    for k in range(len(steps) + 1):
                        if k < len(steps) and steps[k][0] == "head":
                            exp(k)
                        if k:
                            hi(k - 1)
                    act.wait_ge(s["round_done"], b + 2)

            @block.tensor
            def _(pe):
                with pe.Fori(0, B) as b:
                    pe.wait_ge(s["k_loaded"], b * 32 + 32)

                    def score(n):
                        if n >= HEADS:
                            return
                        _, t, h = steps[heads[n]]
                        if h == 0:
                            pe.wait_ge(q_loaded[t % 2], b * 128 + (t // 2 + 1) * 64)
                        if n >= 2:
                            pe.wait_ge(s["expd"], n - 1)
                        q = [a[:, h] for a in qT[t % 2]]
                        g = h // (H1 // G1)
                        mm3(pe, s_ps[:, n % 2, 0:CTX], q, [a[:, g, 0:CTX] for a in kT], True, True)
                        w = width(t)
                        q_hi, q_lo = q
                        k_hi, k_lo = [a[:, g, CTX:w] for a in kT]
                        own = s_ps[:, n % 2, CTX:w]
                        pe.matmul(own, q_lo, k_hi, start=True, stop=False)
                        pe.matmul(s_ps[:, n % 2, w - P:w], c["identb"][:], future[:], start=False, stop=False,
                                  skip_group_check=True)
                        pe.matmul(own, q_hi, k_lo, start=False, stop=False)
                        pe.matmul(own, q_hi, k_hi, start=False, stop=True).then_inc(s["scored"], 1)

                    def turn(k):
                        kind, t, h = steps[k]
                        if k:
                            pe.wait_ge(s["t_lo"], k)
                        if kind == "head":
                            n = head_no[k]
                            pe.wait_ge(s["expd"], n + 1)
                            src = [prob[:, n % 2, m * P:m * P + P] for m in range(width(t) // P)]
                        else:
                            pe.wait_ge(s["scaled"], t * 4 + (h + 1) * 2)
                            src = [o[:, (h * 8 + m) * P:(h * 8 + m + 1) * P] for m in range(8)]
                        for m, a in enumerate(src):
                            mm = pe.transpose(t_ps[:, m * P:m * P + P], a, c["ident"][:])
                        mm.then_inc(s["turned"], 1)

                    def weigh(k):
                        kind, t, h = steps[k]
                        if k == 0:
                            pe.wait_ge(s["v_loaded"], b * 32 + 32)
                        pe.wait_ge(s["t_hi"], k + 1)
                        pe.wait_ge(s["t_lo"], k + 1)
                        if kind == "head":
                            quad = t * 4 + h // 4
                            slot = quad + t
                            g = h // (H1 // G1)
                            if h % 4 == 0 and slot >= 2:
                                pe.wait_ge(s["o_out"], slot - 1)
                            blocks = width(t) // P
                            for m in range(blocks):
                                mm = mm3(pe, o_ps[:, slot % 2, (h % 4) * P:(h % 4) * P + P],
                                         [a[:, k % 2, m * P:m * P + P] for a in probT],
                                         [a[:, m, g * P:g * P + P] for a in v], m == 0, m == blocks - 1)
                        else:
                            slot = t * 5 + 4
                            if h == 0:
                                pe.wait_ge(s["o_out"], slot - 1)
                            for m in range(8):
                                mm = mm3(pe, o_ps[:, slot % 2], [a[:, k % 2, m * P:m * P + P] for a in probT],
                                         [a[:, h * 8 + m] for a in wo], h == 0 and m == 0, h == 1 and m == 7)
                        mm.then_inc(s["summed"], 1)

                    score(0)
                    score(1)
                    n = 2
                    for k in range(len(steps)):
                        turn(k)
                        if steps[k][0] == "head":
                            score(n)
                            n += 1
                        if k:
                            weigh(k - 1)
                    weigh(len(steps) - 1)
                    pe.wait_ge(s["round_done"], b + 2)

            @block.vector
            def _(dve):
                step = Chain(dve, s["step_dve"])
                dve.sem_inc(s["round_done"], 1)
                with dve.Fori(0, B) as b:
                    step.restart()

                    def most(n):
                        if n >= HEADS:
                            return
                        _, t, h = steps[heads[n]]
                        u = t % 2
                        if h == 0:
                            dve.wait_ge(q_loaded[u], b * 128 + (t // 2 + 1) * 64)
                            step(dve.tensor_scalar(rs[:, u], r[:, u], SCALE1, None, ALU.mult))
                        dve.wait_ge(s["scored"], n + 1)
                        if n >= 2:
                            dve.wait_ge(s["expd"], n - 1)
                        w = width(t)
                        step(dve.tensor_reduce(mx[:, n % 2:n % 2 + 1], s_ps[:, n % 2, 0:w], AX.X, ALU.max))
                        dve.tensor_scalar(nb[:, n % 2:n % 2 + 1], mx[:, n % 2:n % 2 + 1], rs[:, u, h:h + 1], -1.0,
                                          ALU.mult, ALU.mult).then_inc(s["maxed"], 1)

                    def lo(k):
                        kind, t, _ = steps[k]
                        w = width(t) if kind == "head" else M1
                        dve.wait_ge(s["t_hi"], k + 1)
                        dve.tensor_tensor(probT[1][:, k % 2, 0:w], t_ps[:, 0:w], probT[0][:, k % 2, 0:w].bitcast(F32),
                                          ALU.subtract).then_inc(s["t_lo"], 1)

                    def out(t, quad):
                        slot = t * 5 + quad
                        last = t * (H1 + 2) + quad * 4 + 3
                        dve.wait_ge(s["summed"], last + 1)
                        step(dve.reciprocal(rinv[:, quad * 4:quad * 4 + 4], rsum[:, quad * 4:quad * 4 + 4]))
                        dve.tensor_tensor(o[:, quad * 512:quad * 512 + 512].rearrange("p (h e) -> p h e", h=4),
                                          o_ps[:, slot % 2].rearrange("p (h e) -> p h e", h=4),
                                          rinv[:, quad * 4:quad * 4 + 4].rearrange("p (h e) -> p h e", e=1).to_broadcast([P, 4, HD]),
                                          ALU.mult).then_inc(s["scaled"], 1)
                        dve.wait_ge(s["scaled"], t * 4 + quad + 1)
                        dve.sem_inc(s["o_out"], 1)

                    def add(t):
                        slot = t * 5 + 4
                        dve.wait_ge(s["summed"], (t + 1) * (H1 + 2))
                        step(dve.scalar_tensor_tensor(x[:, t % 2], o_ps[:, slot % 2], gate[:], x[:, t % 2], ALU.mult, ALU.add))
                        dve.sem_inc(s["o_out"], 1)
                        dve.sem_inc(s["x_ready"], 1)

                    most(0)
                    n = 1
                    for k in range(len(steps)):
                        if n < HEADS and (steps[k][0] == "head"):
                            most(n)
                            n += 1
                        if k >= 2:
                            kind, t, h = steps[k - 2]
                            if kind == "head" and h % 4 == 3:
                                out(t, h // 4)
                            if kind == "o" and h == 1:
                                add(t)
                        lo(k)
                    add(NT - 1)
                    clear_all(dve, of_round)
                    dve.wait_ge(s["stored"], b * (NT * 16) + NT * 16)
                    dve.sem_inc(s["round_done"], 1)
        st.clear()


def split_output_weight(nc, d, c, wo, future, gate):
    with ExitStack() as ctx:
        st = Stage(nc, ctx, "wo1")
        sb, sem = st.sb, st.sem
        full = [sb(f"full{i}", [P, 4, D], F32) for i in range(2)]
        loaded = [sem("loaded0"), sem("loaded1")]
        gate_loaded, gated, split_hi, split_lo, made, filled = (sem(n) for n in "gate_loaded gated split_hi split_lo made filled".split())
        with nc.Block() as block:

            @block.sync
            def _(sp):
                sp.dma_start(gate[:], row_of(d["g_xattn"], 1, 1)).then_inc(gate_loaded, 16)
                for n in range(4):
                    if n >= 2:
                        sp.wait_ge(split_lo, n - 1)
                    sp.dma_start(full[n % 2][:], d["L1_wo"].rearrange("(h p) n -> p h n", p=P)[:, n * 4:n * 4 + 4]).then_inc(loaded[n % 2], 16)

            @block.gpsimd
            def _(pool):
                make_constants(pool, c, made)
                pool.memset(future[:], 0.0).then_inc(filled, 1)
                pool.wait_ge(filled, 1)
                pool.affine_select(out=future[:], in_=future[:], compare_op=ALU.is_ge, fill=BIG, base=0,
                                   pattern=[[-1, P]], channel_multiplier=1).then_inc(filled, 1)

            @block.scalar
            def _(act):
                act.wait_ge(gate_loaded, 16)
                act.activation(gate[:], gate[:], ACT.Tanh).then_inc(gated, 1)
                for n in range(4):
                    act.wait_ge(loaded[n % 2], 16 * (n // 2 + 1))
                    act.activation(wo[0][:, n * 4:n * 4 + 4], full[n % 2][:], ACT.Copy).then_inc(split_hi, 1)

            @block.vector
            def _(dve):
                for n in range(4):
                    dve.wait_ge(split_hi, n + 1)
                    dve.tensor_tensor(wo[1][:, n * 4:n * 4 + 4], full[n % 2][:], wo[0][:, n * 4:n * 4 + 4].bitcast(F32),
                                      ALU.subtract).then_inc(split_lo, 1)
        st.clear()


E = 64
TOP = 8
CAP = P
ROW = D + E
OUT_ROWS = T + CAP


def route(nc, d, x_in, table, out, slots):
    with ExitStack() as ctx:
        st = Stage(nc, ctx, "r1")
        sb, ps, sem = st.sb, st.ps, st.sem
        c = constants(st, nc)
        gate = sb("gate", [P, 1], F32)
        wr = sb("wr", [P, KC, E], F32)
        mhalf4 = sb("mhalf4", [P, NT], F32)
        rank = sb("rank", [P, NT], F32)
        slot_no = sb("slot_no", [E, CAP], F32)
        zeros = sb("zeros", [P, ROW], F32)
        x = [sb(f"x{i}", [P, NT, D], F32) for i in range(2)]
        tab = [sb(f"tab{i}", [P, NT, ROW], F32) for i in range(2)]
        stats, mv = sb("stats", [P, NT, 6], F32), sb("mv", [P, NT, 2], F32)
        ve, rstd = sb("ve", [P, NT], F32), sb("rstd", [P, NT], F32)
        xT = sb("xT", [P, KC, NT * P], F32)
        nmax, total, inv, gs = (sb(n, [P, NT], F32) for n in ("nmax", "total", "inv", "gs"))
        ex, score, left, key = (sb(n, [P, NT, E], F32) for n in ("ex", "score", "left", "key"))
        best = sb("best", [P, NT, TOP], F32)
        keyT = sb("keyT", [E, T], F32)
        first = sb("first", [E, CAP], F32)
        empty = sb("empty", [E, CAP], F32)
        x_ps = [ps(f"x_ps{i}", [P, D], F32) for i in range(NT)]
        logit_ps = ps("logit_ps", [P, NT, E], F32)
        key_ps = ps("key_ps", [E, NT * P], F32)
        slot_ps = ps("slot_ps", [P, E], F32)
        names = ("consts_made consts_loaded gated zero_stored round_done var_ready rstd_ready normed x_turned x_copied "
                 "logits_done maxed expd tab_ready keyed key_turned key_copied firsts_ready slots_turned slots_ready step_dve "
                 "passed_dve passed_sp")
        s = {n: sem(n) for n in names.split()}
        loaded = [sem("loaded0"), sem("loaded1")]
        stored = [sem("stored0"), sem("stored1")]
        of_round = [s[n] for n in ("var_ready rstd_ready normed x_turned x_copied logits_done maxed expd tab_ready "
                                   "keyed key_turned key_copied").split()]
        x_src = x_in[0:T].rearrange("(b t p) d -> b p t d", p=P, t=NT)
        t_dst = table[0:T].rearrange("(b t p) d -> b p t d", p=P, t=NT)

        with nc.Block() as block:

            @block.sync
            def _(sp):
                for to, of in ((wr[:], d["router_wT"].rearrange("(k p) e -> p k e", p=P)), (rank[:], d["rank"]),
                               (slot_no[:], bass.AP(tensor=d["slot_no"].tensor, offset=0, ap=[[0, E], [1, CAP]])),
                               (gate[:], row_of(d["g_ffn"], 1, 1))):
                    sp.dma_start(to, of).then_inc(s["consts_loaded"], 16)
                sp.wait_ge(s["consts_made"], CONSTS + 2)
                sp.dma_start(table[T:], zeros[:]).then_inc(s["zero_stored"], 16)
                sp.dma_start(out[T:], zeros[:, 0:D]).then_inc(s["zero_stored"], 16)
                with sp.Fori(0, B // 2) as n:
                    for u in range(2):
                        sp.dma_start(x[u][:], x_src[n * 2 + u]).then_inc(loaded[u], 16)
                    for u in range(2):
                        sp.wait_ge(s["tab_ready"], u + 1)
                        sp.dma_start(t_dst[n * 2 + u], tab[u][:]).then_inc(stored[u], 16)
                    pass_wait(sp, s["passed_sp"], s["round_done"], n + 1)
                sp.wait_ge(s["zero_stored"], 32)

            @block.gpsimd
            def _(pool):
                make_constants(pool, c, s["consts_made"])
                pool.memset(mhalf4[:], -0.5).then_inc(s["consts_made"], 1)
                pool.memset(zeros[:], 0.0).then_inc(s["consts_made"], 1)
                pool.wait_ge(s["consts_made"], CONSTS + 2)
                with pool.Fori(0, B // 2) as n:
                    for u in range(2):
                        pool.wait_ge(s["var_ready"], u + 1)
                        pool.tensor_tensor(rstd[:], ve[:], mhalf4[:], ALU.pow).then_inc(s["rstd_ready"], 1)
                    pool.wait_ge(s["round_done"], n + 1)

            @block.scalar
            def _(act):
                act.wait_ge(s["consts_loaded"], 64)
                act.activation(gate[:], gate[:], ACT.Tanh).then_inc(s["gated"], 1)
                with act.Fori(0, B // 2) as n:
                    for u in range(2):
                        for t in range(NT):
                            act.wait_ge(s["x_turned"], u * NT + t + 1)
                            act.activation(xT[:, :, t * P:t * P + P], x_ps[t][:].rearrange("p (k n) -> p k n", k=KC),
                                           ACT.Copy).then_inc(s["x_copied"], 1)
                        act.wait_ge(s["maxed"], u + 1)
                        for t in range(NT):
                            act.activation(ex[:, t], logit_ps[:, t], ACT.Exp, bias=nmax[:, t:t + 1],
                                           accum_out=total[:, t:t + 1]).then_inc(s["expd"], 1)
                    act.wait_ge(s["round_done"], n + 1)

            @block.tensor
            def _(pe):
                pe.wait_ge(s["consts_made"], CONSTS)
                pe.wait_ge(s["consts_loaded"], 64)
                with pe.Fori(0, B // 2) as n:
                    for u in range(2):
                        for t in range(NT):
                            pe.wait_ge(s["normed"], u * NT + t + 1)
                            for k in range(KC):
                                mm = pe.transpose(x_ps[t][:, k * P:k * P + P], tab[u][:, t, k * P:k * P + P], c["ident"][:])
                            mm.then_inc(s["x_turned"], 1)
                        if u:
                            pe.wait_ge(s["expd"], u * NT)
                        for t in range(NT):
                            pe.wait_ge(s["x_copied"], u * NT + t + 1)
                            for k in range(KC):
                                mm = pe.matmul(logit_ps[:, t], xT[:, k, t * P:t * P + P], wr[:, k], start=(k == 0),
                                               stop=(k == KC - 1))
                            mm.then_inc(s["logits_done"], 1)
                        pe.wait_ge(s["keyed"], u + 1)
                        for t in range(NT):
                            mm = pe.transpose(key_ps[:, t * P:t * P + P], key[:, t], c["ident"][:])
                        mm.then_inc(s["key_turned"], 1)
                    pe.wait_ge(s["round_done"], n + 1)
                pe.wait_ge(s["firsts_ready"], 1)
                pe.transpose(slot_ps[:], first[:], c["ident"][0:E, 0:E]).then_inc(s["slots_turned"], 1)

            @block.vector
            def _(dve):
                step = Chain(dve, s["step_dve"])

                def wide(a, n):
                    return a.rearrange("p (t e) -> p t e", e=1).to_broadcast([P, NT, n])
                dve.wait_ge(s["gated"], 1)
                with dve.Fori(0, B // 2) as n:
                    step.restart()
                    for u in range(2):
                        dve.wait_ge(loaded[u], n * 16 + 16)
                        for t in range(NT):
                            dve.bn_stats(stats[:, t], x[u][:, t]).then_inc(s["step_dve"], 1)
                        step.n += NT
                        dve.wait_ge(s["step_dve"], step.n)
                        for t in range(NT):
                            dve.bn_aggr(mv[:, t], stats[:, t]).then_inc(s["step_dve"], 1)
                        step.n += NT
                        dve.wait_ge(s["step_dve"], step.n)
                        dve.tensor_scalar(ve[:], mv[:, :, 1], LN_EPS, None, ALU.add).then_inc(s["var_ready"], 1)
                        dve.wait_ge(s["rstd_ready"], u + 1)
                        for t in range(NT):
                            dve.tensor_scalar(tab[u][:, t, 0:D], x[u][:, t], mv[:, t, 0:1], rstd[:, t:t + 1],
                                              ALU.subtract, ALU.mult).then_inc(s["normed"], 1)
                        dve.wait_ge(s["logits_done"], u * NT + NT)
                        step(dve.tensor_reduce(nmax[:], logit_ps[:], AX.X, ALU.max))
                        dve.tensor_scalar(nmax[:], nmax[:], -1.0, None, ALU.mult).then_inc(s["maxed"], 1)
                        dve.wait_ge(s["expd"], u * NT + NT)
                        step(dve.reciprocal(inv[:], total[:]))
                        step(dve.tensor_tensor(score[:], ex[:], wide(inv[:], E), ALU.mult))
                        for t in range(NT):
                            dve.max(best[:, t], score[:, t]).then_inc(s["step_dve"], 1)
                        step.n += NT
                        dve.wait_ge(s["step_dve"], step.n)
                        for t in range(NT):
                            dve.match_replace(left[:, t], best[:, t], score[:, t], -1.0).then_inc(s["step_dve"], 1)
                        dve.tensor_reduce(total[:], best[:], AX.X, ALU.add).then_inc(s["step_dve"], 1)
                        step.n += NT + 1
                        dve.wait_ge(s["step_dve"], step.n)
                        step(dve.tensor_scalar(left[:], left[:], 0.0, None, ALU.is_lt))
                        dve.tensor_tensor(key[:], left[:], wide(rank[:], E), ALU.mult).then_inc(s["keyed"], 1)
                        step(dve.tensor_scalar(total[:], total[:], 1e-20, None, ALU.add))
                        step(dve.reciprocal(inv[:], total[:]))
                        step(dve.tensor_scalar(gs[:], inv[:], gate[:], None, ALU.mult))
                        step(dve.tensor_tensor(tab[u][:, :, D:], score[:], wide(gs[:], E), ALU.mult))
                        dve.sem_inc(s["tab_ready"], 1)
                        dve.wait_ge(s["key_turned"], u + 1)
                        dve.tensor_copy(keyT[:, bass.ds(n * (2 * S) + u * S, S)], key_ps[:]).then_inc(s["key_copied"], 1)
                        step(dve.tensor_scalar(rank[:], rank[:], float(S), None, ALU.subtract))
                    dve.wait_ge(s["key_copied"], 2)
                    dve.wait_ge(s["tab_ready"], 2)
                    for u in range(2):
                        pass_wait(dve, s["passed_dve"], stored[u], n * 16 + 16)
                    clear_all(dve, of_round)
                    dve.sem_inc(s["round_done"], 1)
                step.restart()
                for r in range(CAP // TOP):
                    step(dve.max(first[:, r * TOP:r * TOP + TOP], keyT[:]))
                    step(dve.match_replace(keyT[:], first[:, r * TOP:r * TOP + TOP], keyT[:], 0.0))
                step(dve.tensor_scalar(empty[:], first[:], 0.0, None, ALU.is_equal))
                step(dve.tensor_tensor(empty[:], empty[:], slot_no[:], ALU.mult))
                step(dve.tensor_tensor(first[:], empty[:], first[:], ALU.subtract))
                dve.tensor_scalar(first[:], first[:], float(T), None, ALU.add).then_inc(s["firsts_ready"], 1)
                dve.memset(slots[:, E:], 0)
                dve.wait_ge(s["slots_turned"], 1)
                dve.tensor_copy(slots[:, 0:E], slot_ps[:]).then_inc(s["slots_ready"], 1)
        st.clear()


F1 = 192
FP = F1 // 2
AHEAD = 4


def experts(nc, d, table, out, slots):
    with ExitStack() as ctx:
        st = Stage(nc, ctx, "e1")
        sb, ps, sem = st.sb, st.ps, st.sem
        c = constants(st, nc)
        wgu = [sb(f"wgu{i}", [P, 2, KC, F1], F32) for i in range(AHEAD)]
        wd = [sb(f"wd{i}", [FP, 2, D], F32) for i in range(AHEAD)]
        idx = [sb(f"idx{i}", [P, 1], U32) for i in range(AHEAD)]
        xg = [sb(f"xg{i}", [P, ROW], F32) for i in range(AHEAD)]
        xT = [sb(f"xT{i}", [P, D], F32) for i in range(2)]
        th = [sb(f"th{i}", [FP, 2 * P], F32) for i in range(2)]
        hT = [sb(f"hT{i}", [FP, 2 * P], F32) for i in range(2)]
        yw = [sb(f"yw{i}", [P, D], F32) for i in range(2)]
        x_ps = [ps(f"x_ps{i}", [P, D], F32) for i in range(2)]
        gu_ps = [ps(f"gu_ps{i}", [FP, 4 * P], F32) for i in range(2)]
        y_ps = [ps(f"y_ps{i}", [P, D], F32) for i in range(2)]
        names = ("consts_made passed_pool idx_ready x_turned x_copied gu_done tanhed h_begun h_made y_done scaled "
                 "scattered yw_free")
        s = {n: sem(n) for n in names.split()}
        gathered = [sem(f"gathered{i}") for i in range(AHEAD)]
        w_loaded = [sem(f"w_loaded{i}") for i in range(AHEAD)]
        gu_src = [d[n].rearrange("e (k p) f -> e p k f", p=P) for n in ("w_gate", "w_up")]
        d_src = d["w_down"].rearrange("e (c p) n -> e p c n", p=FP)

        with nc.Block() as block:

            @block.sync
            def _(sp):
                def load(e, u):
                    for i in range(2):
                        sp.dma_start(wgu[u][:, i], gu_src[i][e]).then_inc(w_loaded[u], 16)
                    sp.dma_start(wd[u][:], d_src[e]).then_inc(w_loaded[u], 16)
                for u in range(AHEAD):
                    load(u, u)
                with sp.Fori(0, E // AHEAD - 1) as n:
                    for u in range(AHEAD):
                        wait_apart(sp, s["consts_made"], s["y_done"], n * AHEAD + (u + 1))
                        load(n * AHEAD + (u + AHEAD), u)

            @block.gpsimd
            def _(pool):
                make_constants(pool, c, s["consts_made"])

                def gather(e, i):
                    pool.tensor_copy(idx[i][:], slots[:, bass.ds(e, 1)]).then_inc(s["idx_ready"], 1)
                    pass_wait(pool, s["passed_pool"], s["idx_ready"], e + 1)
                    pool.indirect_dma_start(xg[i][:], None, table[:], bass.IndirectOffsetOnAxis(ap=idx[i][:], axis=0),
                                            bounds_check=OUT_ROWS - 1, compute_op=ALU.bypass).then_inc(gathered[i], 16)
                for e in range(2):
                    pool.tensor_copy(idx[e][:], slots[:, e:e + 1]).then_inc(s["idx_ready"], 1)
                    pool.wait_ge(s["idx_ready"], e + 1)
                    pool.indirect_dma_start(xg[e][:], None, table[:], bass.IndirectOffsetOnAxis(ap=idx[e][:], axis=0),
                                            bounds_check=OUT_ROWS - 1, compute_op=ALU.bypass).then_inc(gathered[e], 16)
                with pool.Fori(0, E // AHEAD) as n:
                    for u in range(AHEAD):
                        pass_wait(pool, s["passed_pool"], s["scaled"], n * AHEAD + (u + 1))
                        gather(n * AHEAD + (u + 2), (u + 2) % AHEAD)
                        pass_wait(pool, s["passed_pool"], s["scaled"], n * AHEAD + (u + 3))
                        pool.indirect_dma_start(out[:], bass.IndirectOffsetOnAxis(ap=idx[u][:], axis=0), yw[u % 2][:], None,
                                                bounds_check=OUT_ROWS - 1, compute_op=ALU.add).then_inc(s["scattered"], 16)
                        pool.wait_ge(s["scattered"], n * (16 * AHEAD) + (u + 1) * 16)
                        pool.sem_inc(s["yw_free"], 1)
                for i in range(2):
                    pool.wait_ge(gathered[i], 16 * (E // AHEAD + 1))

            @block.scalar
            def _(act):
                def copy(e, i):
                    wait_apart(act, s["consts_made"], s["x_turned"], e + 1)
                    act.activation(xT[i][:], x_ps[i][:], ACT.Copy).then_inc(s["x_copied"], 1)
                act.wait_ge(s["x_turned"], 1)
                act.activation(xT[0][:], x_ps[0][:], ACT.Copy).then_inc(s["x_copied"], 1)
                with act.Fori(0, E // AHEAD) as n:
                    for u in range(AHEAD):
                        wait_apart(act, s["consts_made"], s["gu_done"], n * AHEAD + (u + 1))
                        act.activation(th[u % 2][:], gu_ps[u % 2][:, 0:2 * P], ACT.Tanh, scale=0.5).then_inc(s["tanhed"], 1)
                        copy(n * AHEAD + (u + 1), (u + 1) % 2)

            @block.tensor
            def _(pe):
                pe.wait_ge(s["consts_made"], CONSTS)

                def turn(i):
                    for k in range(KC):
                        mm = pe.transpose(x_ps[i % 2][:, k * P:k * P + P], xg[i][:, k * P:k * P + P], c["ident"][:])
                    mm.then_inc(s["x_turned"], 1)
                pe.wait_ge(gathered[0], 16)
                turn(0)
                with pe.Fori(0, E // AHEAD) as n:
                    for u in range(AHEAD):
                        wait_apart(pe, s["consts_made"], s["x_copied"], n * AHEAD + (u + 1))
                        wait_apart(pe, s["consts_made"], w_loaded[u], n * 48 + 48)
                        for which in range(2):
                            for f in range(2):
                                o = (which * 2 + f) * P
                                for k in range(KC):
                                    mm = pe.matmul(gu_ps[u % 2][:, o:o + P], wgu[u][:, which, k, f * FP:f * FP + FP],
                                                   xT[u % 2][:, k * P:k * P + P], start=(k == 0), stop=(k == KC - 1))
                        mm.then_inc(s["gu_done"], 1)
                        wait_apart(pe, s["consts_made"], gathered[(u + 1) % AHEAD], n * 16 + ((u + 1) // AHEAD + 1) * 16)
                        turn((u + 1) % AHEAD)
                        wait_apart(pe, s["consts_made"], s["h_made"], n * AHEAD + (u + 1))
                        wait_apart(pe, s["consts_made"], s["scaled"], n * AHEAD + (u + 1))
                        for f in range(2):
                            mm = pe.matmul(y_ps[u % 2][:], hT[u % 2][:, f * P:f * P + P], wd[u][:, f], start=(f == 0), stop=(f == 1))
                        mm.then_inc(s["y_done"], 1)

            @block.vector
            def _(dve):
                dve.sem_inc(s["scaled"], 2)
                dve.sem_inc(s["yw_free"], 2)

                def inner(e, i):
                    wait_apart(dve, s["consts_made"], s["tanhed"], e + 1)
                    dve.scalar_tensor_tensor(hT[i][:], th[i][:], 1.0, gu_ps[i][:, 0:2 * P], ALU.add, ALU.mult).then_inc(s["h_begun"], 1)
                    wait_apart(dve, s["consts_made"], s["h_begun"], e + 1)
                    dve.scalar_tensor_tensor(hT[i][:], hT[i][:], 0.5, gu_ps[i][:, 2 * P:], ALU.mult, ALU.mult).then_inc(s["h_made"], 1)

                with dve.Fori(0, E // AHEAD) as n:
                    for u in range(AHEAD):
                        inner(n * AHEAD + u, u % 2)
                        wait_apart(dve, s["consts_made"], s["y_done"], n * AHEAD + (u + 1))
                        wait_apart(dve, s["consts_made"], s["yw_free"], n * AHEAD + (u + 1))
                        dve.tensor_scalar(yw[u % 2][:], y_ps[u % 2][:], xg[u][:, bass.ds(n * AHEAD + (D + u), 1)], None,
                                          ALU.mult).then_inc(s["scaled"], 1)
        st.clear()


def layer1_ffn(nc, d, x_in, out):
    with ExitStack() as ctx:
        slots = Stage(nc, ctx, "m1").sb("slots", [P, E + 2], U32)
        table = nc.dram_tensor("token_table", (OUT_ROWS, ROW), F32, kind="Internal").ap()
        route(nc, d, x_in, table, out, slots)
        experts(nc, d, table, out, slots)


def rotary_tables():
    inv = (np.float32(1.0) / np.power(np.float32(10000.0), np.arange(0, 128, 2, dtype=np.float32) / np.float32(128)))
    f = np.outer(np.arange(S, dtype=np.float32), inv.astype(np.float32)).astype(np.float32)
    e = np.concatenate([f, f], 1)
    sign = np.concatenate([-np.ones(64, np.float32), np.ones(64, np.float32)])
    return np.cos(e).astype(np.float32), (np.sin(e) * sign).astype(np.float32)


def program(nc, d, out):
    x1, x2 = (nc.dram_tensor(n, (T, D), F32, kind="Internal").ap() for n in ("x1", "x2"))
    heads = layer1_scratch(nc)
    layer0_attention(nc, d, x1)
    layer0_ffn(nc, d, x1, x2)
    layer1_projections(nc, d, x2, heads)
    layer1_attention(nc, d, x2, heads, out)
    layer1_ffn(nc, d, out, out)


def laid_out(i):
    def t(a):
        return np.ascontiguousarray(np.asarray(a).T)

    def cols(a):
        return np.ascontiguousarray(np.asarray(a).reshape(KC, P).T).reshape(-1)
    cos, sin = rotary_tables()
    return {
        "router_wT": t(i["L1_ffn_router_w"]), "w_gate": i["L1_ffn_w_gate"], "w_up": i["L1_ffn_w_up"],
        "w_down": i["L1_ffn_w_down"],
        "rank": (T - np.arange(S, dtype=np.float32)).reshape(NT, P).T,
        "slot_no": np.arange(CAP, dtype=np.float32),
        "cos": cos, "sin": sin,
        "L1_wq": i["L1_xattn_wq"], "L1_wk": i["L1_xattn_wk"], "L1_wv": i["L1_xattn_wv"], "L1_wo": i["L1_xattn_wo"],
        "L1_wk_ctx": i["L1_xattn_wk_ctx"], "L1_wv_ctx": i["L1_xattn_wv_ctx"],
        "L1_q_norm": i["L1_xattn_q_norm_w"], "L1_k_norm": i["L1_xattn_k_norm_w"],
        "x": i["x"], "mask": i["mask_BxSxS2_ff0"],
        "ctxT": np.ascontiguousarray(np.asarray(i["ctx_2048"]).transpose(0, 2, 1)),
        "g_xattn": i["g_xattn"], "g_ffn": i["g_ffn"],
        "L0_wq": i["L0_xattn_wq"], "L0_wo": i["L0_xattn_wo"],
        "L0_wkT": t(i["L0_xattn_wk"]), "L0_wvT": t(i["L0_xattn_wv"]),
        "L0_bq": cols(i["L0_xattn_bq"]), "L0_bk": cols(i["L0_xattn_bk"]),
        "L0_guT": t(i["L0_ffn_gate_up_packed"]), "L0_gu_scales": i["L0_ffn_gate_up_scales"],
        "L0_dnT": t(i["L0_ffn_down_packed"]), "L0_dn_scales": i["L0_ffn_down_scales"],
        "shifts": (4 * (np.arange(P, dtype=np.int32) % 8)).reshape(P, 1),
        "L0_bv": i["L0_xattn_bv"], "L0_bo": i["L0_xattn_bo"],
    }


def kernel(**inputs):
    import concourse.bacc as bacc
    from concourse.bass_utils import run_bass_kernel_spmd

    nc = bacc.Bacc("TRN2", target_bir_lowering=False, num_devices=1)
    arrays, aps = {}, {}
    for name, a in laid_out(inputs).items():
        a = np.ascontiguousarray(a)
        arrays[f"in_{name}"] = a
        aps[name] = nc.dram_tensor(f"in_{name}", a.shape, mybir.dt.from_np(a.dtype), kind="ExternalInput").ap()
    out = nc.dram_tensor("out_rows", (OUT_ROWS, D), F32, kind="ExternalOutput").ap()
    program(nc, aps, out)
    r = run_bass_kernel_spmd(nc, [arrays], core_ids=[0])
    return r.results[0]["out_rows"][:T].reshape(B, S, D)
```
